# Optimizing a Trainium2 kernel written in Bass

```python
import numpy as np
import jax
import jax.numpy as jnp

def _softmax(x, axis=-1):
    return jax.nn.softmax(x, axis=axis)

def _gelu(x):
    return jax.nn.gelu(x, approximate=True)

def _silu(x):
    return jax.nn.silu(x)

def _sigmoid(x):
    return jax.nn.sigmoid(x)

def _layernorm(x, axis=-1, eps=1e-05):
    m = jnp.mean(x, axis=axis, keepdims=True)
    v = jnp.var(x, axis=axis, keepdims=True)
    return (x - m) / jnp.sqrt(v + eps)

def _scatter_add(tgt, idx, src, axis=0):
    return tgt.at[idx].add(src)

def _segment_sum(src, seg, n):
    return jax.ops.segment_sum(src, seg, n)
kernel_name = 'mk_flamingo_gated_d1_seqx_r4_69a3da'

def setup_inputs(seed: int=0):
    np.random.seed(seed)
    _w = jnp.asarray

    def _rec_inputs():
        import jax
        import jax.numpy as jnp
        _rk = jax.random.key(seed)
        x = -0.000125 + 0.9999 * jax.random.normal(jax.random.fold_in(_rk, 1), (8, 256, 1024), jnp.float32)
        _lenS = 256 - jax.random.randint(jax.random.fold_in(_rk, 7), (8,), 0, max(1, 256 // 4) + 1, jnp.int32)
        _lenS2 = 256 - jax.random.randint(jax.random.fold_in(_rk, 8), (8,), 0, max(1, 256 // 4) + 1, jnp.int32)
        _ctx_4096P = jax.random.normal(jax.random.fold_in(_rk, 11), (8, 16, 1024), jnp.float32)
        _ctx_4096c = jax.random.dirichlet(jax.random.fold_in(_rk, 511), 0.3 * jnp.ones((16,), jnp.float32), (8, 256))
        _ctx_4096t = jnp.einsum('bsk,bkd->bsd', _ctx_4096c, _ctx_4096P)
        _ctx_4096t = _ctx_4096t * jax.lax.rsqrt(jnp.mean(jnp.square(_ctx_4096t)) + 1e-12) * 0.953939
        ctx_4096 = -1.52775e-05 + 0.999936 * (_ctx_4096t + 0.3 * jax.random.normal(jax.random.fold_in(_rk, 611), (8, 256, 1024), jnp.float32))
        _g = jax.random.normal(jax.random.fold_in(_rk, 9001), (2, 1), jnp.float32)
        _g = jnp.sign(_g) * jnp.maximum(jnp.abs(_g), 1.0) + (_g == 0) * 1.0
        g_xattn = _g[0]
        g_ffn = _g[1]
        return (x, ctx_4096, g_xattn, g_ffn)
    x, ctx_4096, g_xattn, g_ffn = _rec_inputs()

    def _L0_xattn_setup():
        import jax, jax.numpy as jnp
        import numpy as np
        B, C, D = (8, 256, 1024)
        GROUPS = 8
        ATTN_SCALE = 1.0
        RESID = 1.0
        EPS = 1e-05
        key = jax.random.key(seed)
        ks = jax.random.split(key, 9)
        s = 1.0 / np.sqrt(C)
        return {'inp_q': jax.random.normal(ks[0], (B, C, D), jnp.float32), 'inp_k': jax.random.normal(ks[1], (B, C, D), jnp.float32), 'inp_v': jax.random.normal(ks[2], (B, C, D), jnp.float32), 'Wt': jax.random.normal(ks[3], (C, C), jnp.float32) * s, 'Wp': jax.random.normal(ks[4], (C, C), jnp.float32) * s, 'Wg': jax.random.normal(ks[5], (C, C), jnp.float32) * s, 'Wz': jax.random.normal(ks[6], (C, C // GROUPS), jnp.float32) * s, 'gn_w': jax.random.normal(ks[7], (C,), jnp.float32), 'gn_b': jax.random.normal(ks[8], (C,), jnp.float32)}
    _L0_xattn_all = _L0_xattn_setup()
    _L0_xattn_in = {k: v for k, v in _L0_xattn_all.items() if k in ('Wt', 'Wp', 'Wg', 'Wz', 'gn_w', 'gn_b')}
    del _L0_xattn_all

    def _L0_ffn_setup():
        import jax, jax.numpy as jnp
        import numpy as np
        IN_F = 1024
        OUT_F = 1024
        RANK = 8
        NUM_EXPERTS = 64
        TOP_K = 16
        ROUTER_DIM = 16
        ALPHA = 32
        SCALING = ALPHA / TOP_K
        BOTTLENECK = NUM_EXPERTS * RANK
        key = jax.random.key(seed)
        ks = jax.random.split(key, 5)
        x = jax.random.normal(ks[0], (4, 1024, IN_F), dtype=jnp.float32)
        bound_a = float(np.sqrt(6.0 / IN_F))
        A_w = jax.random.uniform(ks[1], (BOTTLENECK, IN_F), jnp.float32, -bound_a, bound_a)
        B_w = jax.random.normal(ks[2], (OUT_F, BOTTLENECK), dtype=jnp.float32) * 0.02
        Wq_w = jax.random.normal(ks[3], (ROUTER_DIM, IN_F), dtype=jnp.float32) * 0.02
        keys = jax.random.normal(ks[4], (NUM_EXPERTS, ROUTER_DIM), dtype=jnp.float32) * 0.01
        return {'x': x, 'A_w': A_w, 'B_w': B_w, 'Wq_w': Wq_w, 'keys': keys}
    _L0_ffn_all = _L0_ffn_setup()
    _L0_ffn_in = {k: v for k, v in _L0_ffn_all.items() if k in ('A_w', 'B_w', 'Wq_w', 'keys')}
    del _L0_ffn_all
    return {'x': x, 'ctx_4096': ctx_4096, 'g_xattn': g_xattn, 'g_ffn': g_ffn, 'L0_xattn_Wt': _L0_xattn_in['Wt'], 'L0_xattn_Wp': _L0_xattn_in['Wp'], 'L0_xattn_Wg': _L0_xattn_in['Wg'], 'L0_xattn_Wz': _L0_xattn_in['Wz'], 'L0_xattn_gn_w': _L0_xattn_in['gn_w'], 'L0_xattn_gn_b': _L0_xattn_in['gn_b'], 'L0_ffn_A_w': _L0_ffn_in['A_w'], 'L0_ffn_B_w': _L0_ffn_in['B_w'], 'L0_ffn_Wq_w': _L0_ffn_in['Wq_w'], 'L0_ffn_keys': _L0_ffn_in['keys']}

def reference(x, ctx_4096, g_xattn, g_ffn, L0_xattn_Wt, L0_xattn_Wp, L0_xattn_Wg, L0_xattn_Wz, L0_xattn_gn_w, L0_xattn_gn_b, L0_ffn_A_w, L0_ffn_B_w, L0_ffn_Wq_w, L0_ffn_keys):
    import jax
    import jax.numpy as jnp

    def _L0_xattn_ref(inp_q, inp_k, inp_v, Wt, Wp, Wg, Wz, gn_w, gn_b):
        import jax, jax.numpy as jnp
        import numpy as np
        B, C, D = (8, 256, 1024)
        GROUPS = 8
        ATTN_SCALE = 1.0
        RESID = 1.0
        EPS = 1e-05
        residual = inp_v * RESID
        t = jnp.einsum('oc,bcd->bod', Wt, inp_v)
        p = jnp.einsum('oc,bcd->bod', Wp, inp_q)
        g = jnp.einsum('oc,bcd->bod', Wg, inp_k)
        b, c, d = t.shape
        cg = c // GROUPS
        tg = t.reshape(b, GROUPS, cg * d)
        pg = p.reshape(b, GROUPS, cg * d)
        gg = g.reshape(b, GROUPS, cg * d)
        att = jnp.sum(pg * gg, axis=-1, keepdims=True) * ATTN_SCALE
        x = (att * tg).reshape(b, c, d)
        xg = x.reshape(b, GROUPS, cg, d)
        Wzg = Wz.reshape(GROUPS, cg, cg)
        y = jnp.einsum('goi,bgid->bgod', Wzg, xg).reshape(b, c, d)
        yg = y.reshape(b, GROUPS, cg * d)
        mu = jnp.mean(yg, axis=-1, keepdims=True)
        var = jnp.var(yg, axis=-1, keepdims=True)
        yn = ((yg - mu) * jax.lax.rsqrt(var + EPS)).reshape(b, c, d)
        return yn * gn_w[None, :, None] + gn_b[None, :, None] + residual

    def _L0_ffn_ref(x, A_w, B_w, Wq_w, keys):
        import jax, jax.numpy as jnp
        import numpy as np
        IN_F = 1024
        OUT_F = 1024
        RANK = 8
        NUM_EXPERTS = 64
        TOP_K = 16
        ROUTER_DIM = 16
        ALPHA = 32
        SCALING = ALPHA / TOP_K
        BOTTLENECK = NUM_EXPERTS * RANK
        q = jnp.einsum('bsd,rd->bsr', x, Wq_w)
        scores = jnp.einsum('bsr,er->bse', q, keys)
        top_vals, top_idx = jax.lax.top_k(scores, TOP_K)
        top_w = jax.nn.softmax(top_vals, axis=-1)
        gate = jnp.sum(jax.nn.one_hot(top_idx, NUM_EXPERTS, dtype=top_w.dtype) * top_w[..., None], axis=-2)
        z = jnp.einsum('bsd,nd->bsn', x, A_w)
        z = z.reshape(*z.shape[:-1], NUM_EXPERTS, RANK)
        z_gated = (z * gate[..., None]).reshape(*z.shape[:-2], BOTTLENECK)
        out = jnp.einsum('bsn,on->bso', z_gated, B_w) * SCALING
        return out
    x = x + jnp.tanh(g_xattn[0]) * _L0_xattn_ref(_layernorm(x, axis=-1), ctx_4096, ctx_4096, L0_xattn_Wt, L0_xattn_Wp, L0_xattn_Wg, L0_xattn_Wz, L0_xattn_gn_w, L0_xattn_gn_b)
    x = x + jnp.tanh(g_ffn[0]) * _L0_ffn_ref(_layernorm(x, axis=-1), L0_ffn_A_w, L0_ffn_B_w, L0_ffn_Wq_w, L0_ffn_keys)
    return x

_drawn_inputs = setup_inputs


def setup_inputs(seed=0):
    import zlib

    import numpy as np

    out = dict(_drawn_inputs(seed))
    spreads = {}
    factors = {}
    for name, (base, spread) in spreads.items():
        noise = np.random.default_rng([zlib.crc32(name.encode()), seed]).standard_normal(out[name].shape)
        drawn = base * np.exp(spread * noise) if base else spread * noise
        out[name] = jnp.asarray(drawn.astype(out[name].dtype))
    for name, factor in factors.items():
        out[name] = (out[name] * factor).astype(out[name].dtype)
    return out
```

```python
import concourse.bass as bass
from concourse import mybir
from contextlib import ExitStack


def flamingo_block(nc, x, ctx, g_xattn, g_ffn, Wt, Wp, Wg, Wz, gn_w, gn_b, A_w, B_w, Wq, keys, out):
    f32 = mybir.dt.float32
    f32r = mybir.dt.float32r
    ALU = mybir.AluOpType
    ACT = mybir.ActivationFunctionType

    NB, C, D = x.shape
    P = 128
    T = C // P
    HALF = 512
    NH = D // HALF
    GROUP = Wz.shape[1]
    GPT = P // GROUP
    NN = A_w.shape[0]
    NE, RD = keys.shape
    RANK = NN // NE
    KD = D // P
    KN = NN // P
    ZC = NN + NE
    ZH = ZC // 2
    E0 = ZH // RANK
    E1 = NE - E0
    EPS = 1e-5
    FFN_SCALE = 32 / 16
    TAKEN = -3.0e38
    USES = T * NH

    x_v = x.rearrange("b (t p) d -> b p t d", p=P)
    c_v = ctx.rearrange("b (t p) d -> b p t d", p=P)
    o_v = out.rearrange("b (t p) d -> b t p d", p=P)
    a_v = A_w.rearrange("(s p) d -> s p d", p=P)
    b_v = B_w.rearrange("(s t p) n -> s p t n", p=P, t=2)

    def sample(view, b):
        if isinstance(b, int):
            return view[b]
        return view[bass.ds(b, 1)].rearrange("a p t d -> (a p) t d")

    def tile_of(view, b, t):
        if isinstance(b, int):
            return view[b, t]
        return view[bass.ds(b, 1), t].rearrange("a p d -> (a p) d")

    with ExitStack() as stack:
        def sb(name, shape, dt=f32):
            return stack.enter_context(nc.sbuf_tensor(name, shape, dt))

        def sem(name):
            return stack.enter_context(nc.semaphore(name))

        def sems(name, n):
            return [sem(f"{name}{i}") for i in range(n)]

        A_hi, A_lo = sb("A_hi", [P, KD, ZC], f32r), sb("A_lo", [P, KD, ZC], f32r)
        B_hi, B_lo = sb("B_hi", [P, KN, D], f32r), sb("B_lo", [P, KN, D], f32r)
        Wp_hi, Wp_lo = sb("Wp_hi", [P, T, C], f32r), sb("Wp_lo", [P, T, C], f32r)
        Wg_hi, Wg_lo = sb("Wg_hi", [P, T, C], f32r), sb("Wg_lo", [P, T, C], f32r)
        Wu_hi, Wu_lo = sb("Wu_hi", [P, T, C], f32r), sb("Wu_lo", [P, T, C], f32r)
        x_sb, c_sb = sb("x_sb", [P, T, D]), sb("c_sb", [P, T, D])
        c_hi, c_lo = sb("c_hi", [P, T, D], f32r), sb("c_lo", [P, T, D], f32r)
        q_hi, q_lo = sb("q_hi", [P, T, D], f32r), sb("q_lo", [P, T, D], f32r)
        ln_sb = sb("ln_sb", [P, T, D])
        uw_sb = sb("uw_sb", [P, T, D])
        xt_sb = sb("xt_sb", [P, T, D])
        res_sb = sb("res_sb", [P, T, D])
        o_sb = sb("o_sb", [P, T, D])
        p_sb = sb("p_sb", [P, 2, HALF])
        hT_hi, hT_lo = sb("hT_hi", [P, T, KD * P], f32r), sb("hT_lo", [P, T, KD * P], f32r)
        zg_sb = sb("zg_sb", [P, T, NN])
        zT_hi, zT_lo = sb("zT_hi", [P, T, KN * P], f32r), sb("zT_lo", [P, T, KN * P], f32r)
        stage = sb("stage", [P, D])
        ident, group_mean = sb("ident", [P, P]), sb("group_mean", [P, P])
        minus_half = sb("minus_half", [P, T])
        gates, tg, tg2 = sb("gates", [P, 2]), sb("tg", [P, 2]), sb("tg2", [P, 1])
        gnw, gnb = sb("gnw", [P, T]), sb("gnb", [P, T])
        gnw_t, gnb_t = sb("gnw_t", [P, T]), sb("gnb_t", [P, T])
        x_st, x_mv = sb("x_st", [P, T, NH * 6]), sb("x_mv", [P, T, 2])
        x_ve, x_rs = sb("x_ve", [P, T]), sb("x_rs", [P, T])
        u_st, u_mv = sb("u_st", [P, T, NH * 6]), sb("u_mv", [P, T, 2])
        w_st, w_mv = sb("w_st", [P, T, NH * 6]), sb("w_mv", [P, T, 2])
        w_ve, w_rs = sb("w_ve", [P, T]), sb("w_rs", [P, T])
        g_mean, u_dev = sb("g_mean", [P, T]), sb("u_dev", [P, T])
        att_half, att_var = sb("att_half", [P, T]), sb("att_var", [P, 2 * T])
        va, att, a2 = sb("va", [P, 2 * T]), sb("att", [P, T]), sb("a2", [P, T])
        y_ve, y_rs = sb("y_ve", [P, T]), sb("y_rs", [P, T])
        slope, shift = sb("slope", [P, T]), sb("shift", [P, T])
        sc, sc1, sc2 = sb("sc", [P, NE]), sb("sc1", [P, NE]), sb("sc2", [P, NE])
        top_a, top_b, neg_max = sb("top_a", [P, 8]), sb("top_b", [P, 8]), sb("neg_max", [P, 1])
        ex, eg = sb("ex", [P, NE]), sb("eg", [P, NE])
        g_sum, g_rec = sb("g_sum", [P, 1]), sb("g_rec", [P, 1])

        half = T * C
        wp_nat = o_sb[:, 0, 0:half].rearrange("p (t c) -> p t c", t=T)
        wg_nat = o_sb[:, 0, half:2 * half].rearrange("p (t c) -> p t c", t=T)
        wt_nat = o_sb[:, 1, 0:half].rearrange("p (t c) -> p t c", t=T)
        wz_nat = o_sb[:, 1, half:half + T * P].rearrange("p (t m) -> p t m", t=T)
        wq_nat = zg_sb[0:RD, :, :].rearrange("r t n -> r (t n)")
        keys_nat = p_sb[0:NE, 0, 0:RD]
        wzT = p_sb[:, 1, 0:T * P].rearrange("p (t o) -> p t o", t=T)
        keysT = p_sb[0:RD, 1, T * P:T * P + NE]
        lots = [stage[:, :], res_sb[:, 0, :], res_sb[:, 1, :]]
        N_LOTS = KN + KD // 2

        z_ps = [stack.enter_context(nc.psum_tensor(f"z_ps{i}", [P, HALF], f32)) for i in range(2)]
        t_ps = [stack.enter_context(nc.psum_tensor(f"t_ps{i}", [P, HALF], f32)) for i in range(2)]
        w_ps = [stack.enter_context(nc.psum_tensor(f"w_ps{i}", [P, HALF], f32)) for i in range(4)]

        x_in, c_in, gates_in, wz_in, wt_in = sem("x_in"), sem("c_in"), sem("gates_in"), sem("wz_in"), sem("wt_in")
        wp_in, wg_in, keys_in, wq_in, gn_in = sem("wp_in"), sem("wg_in"), sem("keys_in"), sem("wq_in"), sem("gn_in")
        lot_in = sems("lot_in", N_LOTS)
        o_free = sems("o_free", T)
        pool_set, consts, wz_zero, tanh_done, small_done = (
            sem("pool_set"), sem("consts"), sem("wz_zero"), sem("tanh_done"), sem("small_done"))
        prep_done, prep_hi, prep_lo = sem("prep_done"), sem("prep_hi"), sem("prep_lo")
        x_var, x_rstd, xt_done, q_done, q_hi_s, q_lo_s = (
            sem("x_var"), sem("x_rstd"), sem("xt_done"), sems("q_done", T), sems("q_hi_s", T), sem("q_lo_s"))
        c_hi_s, c_lo_s = sems("c_hi_s", T), sem("c_lo_s")
        u_done, u_copied = sems("u_done", USES), sems("u_copied", USES)
        p_done, p_copied = sems("p_done", USES), sems("p_copied", USES)
        g_done, g_reduced = sems("g_done", USES), sems("g_reduced", USES)
        u_stats, mean_sum, mean_read = sem("u_stats"), sem("mean_sum"), sem("mean_read")
        va_sum, va_read, y_var, y_rstd = sem("va_sum"), sem("va_read"), sem("y_var"), sem("y_rstd")
        w_var, w_rstd, h_done = sems("w_var", T), sems("w_rstd", T), sems("h_done", T)
        hT_done, hT_hi_s, hT_lo_s = sems("hT_done", 2 * T), sems("hT_hi_s", 2 * T), sems("hT_lo_s", 2 * T)
        res_done = sem("res_done")
        z_done, max_done, exp_done, zg_done = (
            sems("z_done", T), sems("max_done", T), sems("exp_done", T), sems("zg_done", T))
        zT_done, zT_hi_s, zT_lo_s = sems("zT_done", T), sems("zT_hi_s", T), sems("zT_lo_s", T)
        out_done, out_added = sems("out_done", USES), sems("out_added", USES)
        dve_step = sem("dve_step")

        stack.enter_context(nc.allow_non_contiguous_dma(reason="norm weights and gates: a few hundred bytes"))
        block = stack.enter_context(nc.Block())

        SMALL = ["wp", "wg", "wz", "wu", "keys", "router"]
        A_GROUPS = [("a", n, g) for n in range(KN) for g in range(KD // 4)]
        B_GROUPS = [("b", o, 0) for o in range(KD)]
        n_small, n_a, n_b = len(SMALL), len(A_GROUPS), len(B_GROUPS)
        PREP = [(s, 0, 0) for s in SMALL] + A_GROUPS + B_GROUPS
        LOT_DONE = [n_small + 2 * j + 2 for j in range(N_LOTS)]

        def prep_dest(n):
            kind, i, g = PREP[n]
            ps = t_ps[n % 2]
            whole = ps[:, 0:half].rearrange("p (t c) -> p t c", t=T)
            if kind == "wp":
                return whole, Wp_hi[:, :, :], Wp_lo[:, :, :]
            if kind == "wg":
                return whole, Wg_hi[:, :, :], Wg_lo[:, :, :]
            if kind == "wu":
                return whole, Wu_hi[:, :, :], Wu_lo[:, :, :]
            if kind == "wz":
                return ps[:, 0:T * P].rearrange("p (t o) -> p t o", t=T), wzT, None
            if kind == "keys":
                return ps[0:RD, 0:NE], keysT, None
            if kind == "router":
                cols = slice(NN, NN + NE)
                return ps[:, :].rearrange("p (k e) -> p k e", k=KD), A_hi[:, :, cols], A_lo[:, :, cols]
            four = ps[:, :].rearrange("p (k n) -> p k n", k=4)
            if kind == "a":
                at = (slice(None), slice(4 * g, 4 * g + 4), slice(i * P, i * P + P))
                return four, A_hi[at], A_lo[at]
            at = (slice(None), slice(0, KN), slice(i * P, i * P + P))
            return four, B_hi[at], B_lo[at]

        @block.sync
        def _(sp):
            sp.dma_start(x_sb[:, :, :], sample(x_v, 0)).then_inc(x_in, 16)
            sp.dma_start(c_sb[:, :, :], sample(c_v, 0)).then_inc(c_in, 16)
            sp.dma_start(gates[:, 0:1], g_xattn.partition_broadcast(P)).then_inc(gates_in, 16)
            sp.dma_start(gates[:, 1:2], g_ffn.partition_broadcast(P)).then_inc(gates_in, 16)
            sp.dma_start(wt_nat, Wt.rearrange("(t p) c -> p t c", p=P)).then_inc(wt_in, 16)
            sp.dma_start(wp_nat, Wp.rearrange("(t p) c -> p t c", p=P)).then_inc(wp_in, 16)
            sp.dma_start(wg_nat, Wg.rearrange("(t p) c -> p t c", p=P)).then_inc(wg_in, 16)
            sp.wait_ge(wz_zero, 1)
            for g in range(GPT):
                rows = slice(g * GROUP, g * GROUP + GROUP)
                sp.dma_start(wz_nat[rows, :, rows],
                             Wz.rearrange("(t g o) i -> g o t i", t=T, g=GPT)[g]).then_inc(wz_in, 16)
            sp.dma_start(keys_nat, keys).then_inc(keys_in, 16)
            sp.dma_start(wq_nat, Wq).then_inc(wq_in, 16)

            def load_lot(j):
                place = lots[j % len(lots)]
                if j >= len(lots):
                    sp.wait_ge(prep_done, LOT_DONE[j - len(lots)])
                if j < KN:
                    sp.dma_start(place, a_v[j]).then_inc(lot_in[j], 16)
                else:
                    sp.dma_start(place.rearrange("p (t n) -> p t n", t=2), b_v[j - KN]).then_inc(lot_in[j], 16)

            for j in range(len(lots)):
                load_lot(j)
            sp.dma_start(gnw[:, :], gn_w.rearrange("(t p) -> p t", p=P)).then_inc(gn_in, 16)
            sp.dma_start(gnb[:, :], gn_b.rearrange("(t p) -> p t", p=P)).then_inc(gn_in, 16)
            for j in range(len(lots), N_LOTS):
                load_lot(j)

            def load(b, n_prev):
                sp.wait_ge(xt_done, n_prev)
                sp.wait_ge(c_lo_s, n_prev)
                sp.dma_start(x_sb[:, :, :], sample(x_v, b)).then_inc(x_in, 16)
                sp.dma_start(c_sb[:, :, :], sample(c_v, b)).then_inc(c_in, 16)

            def store(b, n):
                for t in range(T):
                    sp.wait_ge(out_added[NH * t + NH - 1], n + 1)
                    sp.dma_start(tile_of(o_v, b, t), o_sb[:, t, :]).then_inc(o_free[t], 16)

            load(1, 1)
            with sp.Fori(0, NB - 2) as b:
                load(b + 2, sp.snap(b + 2))
                store(b, b + 1)
            for b in range(NB - 2, NB):
                store(b, b + 1)
            for t in range(T):
                sp.wait_ge(o_free[t], 16 * (NB + 1))

        @block.gpsimd
        def _(pool):
            pool.memset(ident[:, :], 0.0).then_inc(pool_set, 1)
            pool.memset(minus_half[:, :], -0.5).then_inc(pool_set, 1)
            pool.wait_ge(pool_set, 2)
            pool.affine_select(out=ident[:, :], in_=ident[:, :], compare_op=ALU.not_equal, fill=1.0,
                               base=0, pattern=[[-1, P]], channel_multiplier=1).then_inc(consts, 1)

            def attention(n, prev):
                for t in range(T):
                    pool.wait_ge(c_hi_s[t], n)
                    if prev is not None:
                        pool.wait_ge(g_done[USES - 1], prev)
                    last = pool.tensor_tensor(c_lo[:, t, :], c_sb[:, t, :], c_hi[:, t, :].bitcast(f32),
                                              ALU.subtract)
                last.then_inc(c_lo_s, 1)
                pool.wait_ge(x_var, n)
                pool.tensor_tensor(x_rs[:, :], x_ve[:, :], minus_half[:, :], ALU.pow).then_inc(x_rstd, 1)
                for t in range(T):
                    pool.wait_ge(q_hi_s[t], n)
                    last = pool.tensor_tensor(q_lo[:, t, :], ln_sb[:, t, :], q_hi[:, t, :].bitcast(f32),
                                              ALU.subtract)
                last.then_inc(q_lo_s, 1)
                pool.wait_ge(y_var, n)
                pool.tensor_tensor(y_rs[:, :], y_ve[:, :], minus_half[:, :], ALU.pow).then_inc(y_rstd, 1)
                for t in range(T):
                    pool.wait_ge(w_var[t], n)
                    pool.tensor_tensor(w_rs[:, t:t + 1], w_ve[:, t:t + 1], minus_half[:, t:t + 1],
                                       ALU.pow).then_inc(w_rstd[t], 1)

            attention(1, None)
            with pool.Fori(0, NB - 1) as b:
                attention(pool.snap(b + 2), pool.snap(b + 1))

        @block.scalar
        def _(act):
            def prep(n):
                src, hi, lo = prep_dest(n)
                act.wait_ge(prep_done, n + 1)
                act.activation(hi, src, ACT.Copy).then_inc(prep_hi, 1)

            def ctx_hi(n, prev):
                act.wait_ge(c_in, 16 if prev is None else act_c_in)
                if prev is not None:
                    act.wait_ge(g_done[USES - 1], prev)
                for t in range(T):
                    act.activation(c_hi[:, t, :], c_sb[:, t, :], ACT.Copy).then_inc(c_hi_s[t], 1)

            def query_hi(n):
                for t in range(T):
                    act.wait_ge(q_done[t], n)
                    act.activation(q_hi[:, t, :], ln_sb[:, t, :], ACT.Copy).then_inc(q_hi_s[t], 1)

            def residual(n):
                act.wait_ge(h_done[T - 1], n)
                act.wait_ge(out_added[USES - 1], n)
                for t in range(T):
                    last = act.activation(res_sb[:, t, :], uw_sb[:, t, :], ACT.Identity, bias=shift[:, t:t + 1])
                last.then_inc(res_done, 1)

            def u_copy(k, n):
                t, h = divmod(k, NH)
                act.wait_ge(u_done[k], n)
                act.activation(uw_sb[:, t, h * HALF:(h + 1) * HALF], w_ps[k][:, :], ACT.Copy).then_inc(u_copied[k], 1)

            def p_copy(k, n):
                act.wait_ge(p_done[k], n)
                if k >= 2:
                    act.wait_ge(g_reduced[k - 2], n)
                act.activation(p_sb[:, k % 2, :], w_ps[2 * (k % 2)][:, :], ACT.Copy).then_inc(p_copied[k], 1)

            def hT_high(t, n):
                for g in range(2):
                    k = 2 * t + g
                    act.wait_ge(hT_done[k], n)
                    act.activation(hT_hi[:, t, g * HALF:(g + 1) * HALF], t_ps[g][:, :], ACT.Copy)\
                       .then_inc(hT_hi_s[k], 1)

            def zT_high(t, n):
                act.wait_ge(zT_done[t], n)
                act.activation(zT_hi[:, t, :], t_ps[0][:, :], ACT.Copy).then_inc(zT_hi_s[t], 1)

            def exps(t, n):
                act.wait_ge(max_done[t], n)
                act.activation(ex[:, :], sc[:, :], ACT.Exp, bias=neg_max[:, 0:1]).then_inc(exp_done[t], 1)

            act.wait_ge(gates_in, 32)
            act.activation(tg[:, :], gates[:, :], ACT.Tanh).then_inc(tanh_done, 1)
            ctx_hi(1, None)
            for n in range(n_small):
                prep(n)
            query_hi(1)
            for k in range(USES):
                u_copy(k, 1)
                prep(n_small + 2 * k)
                prep(n_small + 2 * k + 1)
            for k in range(USES):
                p_copy(k, 1)
                prep(n_small + n_a + 2 * k)
                prep(n_small + n_a + 2 * k + 1)
            hT_high(0, 1)

            def ffn_and_next(n, m):
                ctx_hi(m, n)
                residual(n)
                hT_high(1, n)
                exps(0, n)
                act.wait_ge(res_done, n)
                for k in range(USES):
                    u_copy(k, m)
                zT_high(0, n)
                query_hi(m)
                exps(1, n)
                for k in range(USES):
                    p_copy(k, m)
                    if k == 2:
                        zT_high(1, n)
                hT_high(0, m)

            with act.Fori(0, NB - 1) as b:
                act_c_in = act.snap(16 * b + 32)
                ffn_and_next(act.snap(b + 1), act.snap(b + 2))
            residual(NB)
            hT_high(1, NB)
            exps(0, NB)
            zT_high(0, NB)
            exps(1, NB)
            zT_high(1, NB)

        @block.vector
        def _(dve):
            steps = [0]

            def step(instruction):
                instruction.then_inc(dve_step, 1)
                steps[0] += 1

            def settle():
                dve.wait_ge(dve_step, steps[0])

            def fresh_steps():
                settle()
                dve.sem_clear(dve_step)
                steps[0] = 0

            def prep(n):
                src, hi, lo = prep_dest(n)
                dve.wait_ge(prep_hi, n + 1)
                if lo is None:
                    dve.engine_nop().then_inc(prep_lo, 1)
                    return
                dve.tensor_tensor(lo, src, hi.bitcast(f32), ALU.subtract).then_inc(prep_lo, 1)

            def x_stats(n, n_dma):
                dve.wait_ge(x_in, n_dma)
                for t in range(T):
                    for h in range(NH):
                        step(dve.bn_stats(x_st[:, t, 6 * h:6 * h + 6], x_sb[:, t, h * HALF:(h + 1) * HALF]))
                settle()
                for t in range(T):
                    step(dve.bn_aggr(x_mv[:, t, :], x_st[:, t, :]))
                settle()
                dve.tensor_scalar(x_ve[:, :], x_mv[:, :, 1], EPS, None, ALU.add).then_inc(x_var, 1)

            def x_plus_ctx(n, n_dma):
                dve.wait_ge(c_in, n_dma)
                for t in range(T):
                    last = dve.scalar_tensor_tensor(xt_sb[:, t, :], c_sb[:, t, :], tg[:, 0:1], x_sb[:, t, :],
                                                    ALU.mult, ALU.add)
                last.then_inc(xt_done, 1)

            def query(n, prev):
                dve.wait_ge(x_rstd, n)
                if prev is not None:
                    dve.wait_ge(hT_done[2 * T - 1], prev)
                for t in range(T):
                    dve.tensor_scalar(ln_sb[:, t, :], x_sb[:, t, :], x_mv[:, t, 0:1], x_rs[:, t:t + 1],
                                      ALU.subtract, ALU.mult).then_inc(q_done[t], 1)

            def gate(t, n):
                dve.wait_ge(z_done[t], n)
                step(dve.tensor_copy(sc[:, :], z_ps[1][:, ZH - NE:ZH]))
                settle()
                step(dve.max(top_a[:, :], sc[:, :]))
                settle()
                dve.tensor_scalar(neg_max[:, :], top_a[:, 0:1], -1.0, None, ALU.mult).then_inc(max_done[t], 1)
                step(dve.match_replace(sc1[:, :], top_a[:, :], sc[:, :], TAKEN))
                settle()
                step(dve.max(top_b[:, :], sc1[:, :]))
                settle()
                step(dve.match_replace(sc2[:, :], top_b[:, :], sc1[:, :], TAKEN))
                settle()
                dve.wait_ge(exp_done[t], n)
                step(dve.scalar_tensor_tensor(eg[:, :], sc2[:, :], TAKEN, ex[:, :], ALU.is_equal, ALU.mult,
                                              accum_out=g_sum[:, :]))
                settle()
                step(dve.reciprocal(g_rec[:, :], g_sum[:, :]))
                settle()
                for i, (e, k) in enumerate(((0, E0), (E0, E1))):
                    last = dve.scalar_tensor_tensor(
                        zg_sb[:, t, e * RANK:(e + k) * RANK].rearrange("p (e r) -> p e r", r=RANK),
                        z_ps[i][:, 0:k * RANK].rearrange("p (e r) -> p e r", r=RANK), g_rec[:, :],
                        eg[:, e:e + k].unsqueeze(2).to_broadcast([P, k, RANK]), ALU.mult, ALU.mult)
                last.then_inc(zg_done[t], 1)

            def hT_low(t, n):
                for g in range(2):
                    k = 2 * t + g
                    at = (slice(None), t, slice(g * HALF, (g + 1) * HALF))
                    dve.wait_ge(hT_hi_s[k], n)
                    dve.tensor_tensor(hT_lo[at], t_ps[g][:, :], hT_hi[at].bitcast(f32), ALU.subtract)\
                       .then_inc(hT_lo_s[k], 1)

            def zT_low(t, n):
                dve.wait_ge(zT_hi_s[t], n)
                dve.tensor_tensor(zT_lo[:, t, :], t_ps[0][:, :], zT_hi[:, t, :].bitcast(f32), ALU.subtract)\
                   .then_inc(zT_lo_s[t], 1)

            def u_statistics(n):
                for k in range(USES):
                    t, h = divmod(k, NH)
                    dve.wait_ge(u_copied[k], n)
                    step(dve.bn_stats(u_st[:, t, 6 * h:6 * h + 6], uw_sb[:, t, h * HALF:(h + 1) * HALF]))
                settle()
                for t in range(T):
                    last = dve.bn_aggr(u_mv[:, t, :], u_st[:, t, :])
                last.then_inc(u_stats, 1)

            def group_deviation(n):
                dve.wait_ge(mean_sum, n)
                dve.tensor_copy(g_mean[:, :], t_ps[1][:, 0:T]).then_inc(mean_read, 1)
                dve.wait_ge(mean_read, n)
                step(dve.tensor_tensor(u_dev[:, :], u_mv[:, :, 0], g_mean[:, :], ALU.subtract))
                settle()
                step(dve.tensor_tensor(a2[:, :], u_dev[:, :], u_dev[:, :], ALU.mult))
                settle()
                step(dve.tensor_tensor(att_var[:, T:2 * T], a2[:, :], u_mv[:, :, 1], ALU.add))

            def reduce_pg(k, n):
                t, h = divmod(k, NH)
                into = att_half[:, t:t + 1] if h == 0 else att_var[:, t:t + 1]
                dve.wait_ge(p_copied[k], n)
                if h > 0:
                    dve.wait_ge(g_reduced[k - 1], n)
                dve.wait_ge(g_done[k], n)
                dve.tensor_tensor_reduce(out=p_sb[:, k % 2, :], in0=w_ps[2 * (k % 2) + 1][:, :],
                                         in1=p_sb[:, k % 2, :], scale=1.0,
                                         scalar=0.0 if h == 0 else att_half[:, t:t + 1],
                                         op0=ALU.mult, op1=ALU.add, accum_out=into).then_inc(g_reduced[k], 1)

            def slopes(n, meanwhile):
                dve.wait_ge(va_sum, n)
                dve.tensor_copy(va[:, :], t_ps[1][:, 0:2 * T]).then_inc(va_read, 1)
                dve.wait_ge(va_read, n)
                step(dve.tensor_scalar(att[:, :], va[:, 0:T], float(GROUP), None, ALU.mult))
                settle()
                step(dve.tensor_tensor(a2[:, :], att[:, :], att[:, :], ALU.mult))
                settle()
                step(dve.tensor_tensor(a2[:, :], a2[:, :], va[:, T:2 * T], ALU.mult))
                step(dve.tensor_tensor(att[:, :], att[:, :], gnw_t[:, :], ALU.mult))
                settle()
                dve.tensor_scalar(y_ve[:, :], a2[:, :], EPS, None, ALU.add).then_inc(y_var, 1)
                meanwhile()
                dve.wait_ge(y_rstd, n)
                step(dve.tensor_tensor(slope[:, :], att[:, :], y_rs[:, :], ALU.mult))
                settle()

            def w_tile(t, meanwhile=None):
                step(dve.scalar_tensor_tensor(uw_sb[:, t, :], uw_sb[:, t, :], slope[:, t:t + 1], xt_sb[:, t, :],
                                              ALU.mult, ALU.add))
                settle()
                for h in range(NH):
                    step(dve.bn_stats(w_st[:, t, 6 * h:6 * h + 6], uw_sb[:, t, h * HALF:(h + 1) * HALF]))
                if meanwhile:
                    meanwhile()
                settle()
                step(dve.bn_aggr(w_mv[:, t, :], w_st[:, t, :]))
                settle()
                dve.tensor_scalar(w_ve[:, t:t + 1], w_mv[:, t, 1:2], EPS, None, ALU.add).then_inc(w_var[t], 1)

            def shifts():
                step(dve.tensor_tensor(shift[:, :], g_mean[:, :], slope[:, :], ALU.mult))
                settle()
                step(dve.tensor_tensor(shift[:, :], gnb_t[:, :], shift[:, :], ALU.subtract))

            def h_tile(t, n):
                dve.wait_ge(w_rstd[t], n)
                dve.wait_ge(q_lo_s, n)
                dve.tensor_scalar(ln_sb[:, t, :], uw_sb[:, t, :], w_mv[:, t, 0:1], w_rs[:, t:t + 1],
                                  ALU.subtract, ALU.mult).then_inc(h_done[t], 1)

            def finish_attention(n, add=lambda k: None):
                slopes(n, lambda: add(0))
                w_tile(0)
                shifts()
                add(1)
                h_tile(0, n)
                w_tile(1, lambda: hT_low(0, n))
                add(2)
                h_tile(1, n)
                add(3)

            def add_out(k, n, n_dma):
                t, h = divmod(k, NH)
                cols = slice(h * HALF, (h + 1) * HALF)
                if h == 0:
                    dve.wait_ge(o_free[t], n_dma)
                if k == 0:
                    dve.wait_ge(res_done, n)
                dve.wait_ge(out_done[k], n)
                dve.scalar_tensor_tensor(o_sb[:, t, cols], w_ps[k][:, :], tg2[:, 0:1], res_sb[:, t, cols],
                                         ALU.mult, ALU.add).then_inc(out_added[k], 1)

            dve.memset(wz_nat, 0.0).then_inc(wz_zero, 1)
            step(dve.memset(group_mean[:, :], 0.0))
            settle()
            for g in range(GPT):
                rows = slice(g * GROUP, g * GROUP + GROUP)
                dve.memset(group_mean[rows, rows], 1.0 / GROUP).then_inc(consts, 1)
            x_stats(1, 16)
            dve.wait_ge(tanh_done, 1)
            query(1, None)
            x_plus_ctx(1, 16)
            for n in range(n_small):
                prep(n)
            for k in range(USES):
                prep(n_small + 2 * k)
                prep(n_small + 2 * k + 1)
            u_statistics(1)
            dve.wait_ge(gn_in, 32)
            step(dve.tensor_scalar(gnw_t[:, :], gnw[:, :], tg[:, 0:1], None, ALU.mult))
            step(dve.tensor_scalar(gnb_t[:, :], gnb[:, :], tg[:, 0:1], None, ALU.mult))
            step(dve.tensor_scalar(tg2[:, :], tg[:, 1:2], FFN_SCALE, None, ALU.mult))
            group_deviation(1)
            for k in range(USES):
                prep(n_small + n_a + 2 * k)
                reduce_pg(k, 1)
                prep(n_small + n_a + 2 * k + 1)
            finish_attention(1)
            fresh_steps()

            def ffn_and_next(n, m, n_dma, m_dma):
                x_stats(m, m_dma)
                hT_low(1, n)
                query(m, n)
                gate(0, n)
                x_plus_ctx(m, m_dma)
                u_statistics(m)
                zT_low(0, n)
                gate(1, n)
                group_deviation(m)
                for k in range(USES):
                    reduce_pg(k, m)
                    if k == 1:
                        zT_low(1, n)
                finish_attention(m, lambda k: add_out(k, n, n_dma))
                fresh_steps()

            with dve.Fori(0, NB - 1) as b:
                ffn_and_next(dve.snap(b + 1), dve.snap(b + 2), dve.snap(16 * b + 16), dve.snap(16 * b + 32))
            hT_low(1, NB)
            gate(0, NB)
            zT_low(0, NB)
            gate(1, NB)
            zT_low(1, NB)
            for k in range(USES):
                add_out(k, NB, 16 * NB)

        @block.tensor
        def _(pe):
            def prep(n):
                kind, i, g = PREP[n]
                ps = t_ps[n % 2]
                if n >= 2:
                    pe.wait_ge(prep_lo, n - 1)
                if kind in ("wp", "wg"):
                    nat, arrived = (wp_nat, wp_in) if kind == "wp" else (wg_nat, wg_in)
                    pe.wait_ge(arrived, 16)
                    for o in range(T):
                        for c in range(T):
                            last = pe.transpose(ps[:, c * C + o * P:c * C + o * P + P],
                                                nat[:, o, c * P:c * P + P], ident[:, :])
                elif kind == "wz":
                    pe.wait_ge(wz_in, 16 * GPT)
                    for o in range(T):
                        last = pe.transpose(ps[:, o * P:o * P + P], wz_nat[:, o, :], ident[:, :])
                elif kind == "wu":
                    pe.wait_ge(wt_in, 16)
                    pe.wait_ge(prep_hi, SMALL.index("wz") + 1)
                    for o in range(T):
                        for c in range(T):
                            last = pe.matmul(ps[:, c * C + o * P:c * C + o * P + P],
                                             wt_nat[:, o, c * P:c * P + P], wzT[:, o, :], start=True, stop=True)
                elif kind == "keys":
                    pe.wait_ge(keys_in, 16)
                    last = pe.transpose(ps[0:RD, 0:NE], keys_nat, ident[0:NE, 0:NE])
                elif kind == "router":
                    pe.wait_ge(wq_in, 16)
                    pe.wait_ge(prep_hi, SMALL.index("keys") + 1)
                    for k in range(KD):
                        last = pe.matmul(ps[:, k * NE:k * NE + NE], wq_nat[:, k * P:k * P + P], keysT,
                                         start=True, stop=True)
                elif kind == "a":
                    pe.wait_ge(lot_in[i], 16)
                    for k in range(4):
                        d = (4 * g + k) * P
                        last = pe.transpose(ps[:, k * P:k * P + P], lots[i % len(lots)][:, d:d + P], ident[:, :])
                else:
                    j = KN + i // 2
                    pe.wait_ge(lot_in[j], 16)
                    for k in range(KN):
                        at = (i % 2) * NN + k * P
                        last = pe.transpose(ps[:, k * P:k * P + P], lots[j % len(lots)][:, at:at + P], ident[:, :])
                last.then_inc(prep_done, 1)

            def product(ps, w_hi, w_lo, v_hi, v_lo, k, ins):
                t, h = divmod(k, NH)
                rows, cols = slice(t * P, t * P + P), slice(h * HALF, (h + 1) * HALF)
                passes = [(w, v, c) for c in range(T) for w, v in ((w_hi, v_hi), (w_hi, v_lo), (w_lo, v_hi))]
                for i, (w, v, c) in enumerate(passes):
                    last = pe.matmul(ps, w[:, c, rows], v[:, c, cols], start=(i == 0), stop=(i == len(passes) - 1))
                last.then_inc(ins, 1)

            def u_product(n, between=None):
                pe.wait_ge(c_lo_s, n)
                for k in range(USES):
                    product(w_ps[k][:, :], Wu_hi, Wu_lo, c_hi, c_lo, k, u_done[k])
                    if between:
                        between(k)

            def pg_products(n, between):
                pe.wait_ge(q_lo_s, n)
                for k in range(USES):
                    first = 2 * (k % 2)
                    pe.wait_ge(u_copied[first] if k < 2 else p_copied[k - 2], n)
                    product(w_ps[first][:, :], Wp_hi, Wp_lo, q_hi, q_lo, k, p_done[k])
                    between(k, 0)
                    pe.wait_ge(u_copied[first + 1] if k < 2 else g_reduced[k - 2], n)
                    product(w_ps[first + 1][:, :], Wg_hi, Wg_lo, c_hi, c_lo, k, g_done[k])
                    between(k, 1)

            def group_means(n):
                pe.wait_ge(u_stats, n)
                pe.matmul(t_ps[1][:, 0:T], group_mean[:, :], u_mv[:, :, 0], start=True, stop=True)\
                  .then_inc(mean_sum, 1)

            def group_att_var(n):
                pe.wait_ge(mean_read, n)
                pe.wait_ge(g_reduced[USES - 1], n)
                pe.matmul(t_ps[1][:, 0:2 * T], group_mean[:, :], att_var[:, :], start=True, stop=True)\
                  .then_inc(va_sum, 1)

            def hT(t, n):
                pe.wait_ge(h_done[t], n)
                for g in range(2):
                    for k in range(4):
                        d = (4 * g + k) * P
                        last = pe.transpose(t_ps[g][:, k * P:k * P + P], ln_sb[:, t, d:d + P], ident[:, :])
                    last.then_inc(hT_done[2 * t + g], 1)
                    if g == 0:
                        pe.wait_ge(va_read if t == 0 else hT_lo_s[1], n)

            def z_product(t, n, middle=None):
                for k in range(KD):
                    if k % 4 == 0:
                        pe.wait_ge(hT_lo_s[2 * t + k // 4], n)
                    row = slice(k * P, k * P + P)
                    for h, w in ((hT_hi, A_hi), (hT_hi, A_lo), (hT_lo, A_hi)):
                        for i in range(2):
                            last = pe.matmul(z_ps[i][:, 0:ZH], h[:, t, row], w[:, k, i * ZH:(i + 1) * ZH],
                                             start=(k == 0 and h is hT_hi and w is A_hi),
                                             stop=(k == KD - 1 and h is hT_lo))
                    if k == 3 and middle:
                        middle()
                last.then_inc(z_done[t], 1)

            def zT(t, n):
                pe.wait_ge(zg_done[t], n)
                for k in range(KN):
                    last = pe.transpose(t_ps[0][:, k * P:k * P + P], zg_sb[:, t, k * P:k * P + P], ident[:, :])
                last.then_inc(zT_done[t], 1)

            def out_product(k, n, middle=None):
                t, h = divmod(k, NH)
                cols = slice(h * HALF, (h + 1) * HALF)
                pe.wait_ge(zT_lo_s[t], n)
                for j in range(KN):
                    row = slice(j * P, j * P + P)
                    for z, w in ((zT_hi, B_hi), (zT_hi, B_lo), (zT_lo, B_hi)):
                        last = pe.matmul(w_ps[k][:, :], z[:, t, row], w[:, j, cols],
                                         start=(j == 0 and z is zT_hi and w is B_hi),
                                         stop=(j == KN - 1 and z is zT_lo))
                    if j == KN // 2 - 1 and middle:
                        middle()
                last.then_inc(out_done[k], 1)

            for t in range(T):
                pe.sem_inc(o_free[t], 16)
            for k in range(USES):
                pe.sem_inc(out_added[k], 1)
            pe.wait_ge(consts, 1 + GPT)
            for n in range(n_small):
                prep(n)

            def prep_a(k):
                prep(n_small + 2 * k)
                prep(n_small + 2 * k + 1)

            u_product(1, prep_a)
            pe.wait_ge(prep_lo, n_small + n_a)
            group_means(1)
            pe.wait_ge(mean_read, 1)
            pg_products(1, lambda k, i: prep(n_small + n_a + 2 * k + i))
            pe.wait_ge(prep_lo, len(PREP))
            group_att_var(1)
            hT(0, 1)

            def ffn_and_next(n, m):
                def second_tile():
                    pe.wait_ge(hT_lo_s[0], n)
                    hT(1, n)

                z_product(0, n, second_tile)
                u_product_next(n, m)
                pe.wait_ge(hT_lo_s[2], n)
                zT(0, n)
                pe.wait_ge(zg_done[0], n)
                z_product(1, n)
                pe.wait_ge(hT_lo_s[3], n)
                group_means(m)

                def between(k, i):
                    if (k, i) == (2, 0):
                        pe.wait_ge(zT_lo_s[0], n)
                        zT(1, n)

                pg_products(m, between)
                pe.wait_ge(p_copied[2], m)
                out_product(0, n, lambda: group_att_var(m))
                pe.wait_ge(g_reduced[2], m)
                out_product(1, n)
                pe.wait_ge(p_copied[3], m)
                out_product(2, n)
                pe.wait_ge(zT_lo_s[1], n)
                hT(0, m)
                pe.wait_ge(g_reduced[3], m)
                out_product(3, n)

            def u_product_next(n, m):
                pe.wait_ge(c_lo_s, m)
                for k in range(USES):
                    pe.wait_ge(out_added[k], n)
                    product(w_ps[k][:, :], Wu_hi, Wu_lo, c_hi, c_lo, k, u_done[k])

            with pe.Fori(0, NB - 1) as b:
                ffn_and_next(pe.snap(b + 1), pe.snap(b + 2))

            def last_second_tile():
                pe.wait_ge(hT_lo_s[0], NB)
                hT(1, NB)

            z_product(0, NB, last_second_tile)
            pe.wait_ge(hT_lo_s[2], NB)
            zT(0, NB)
            z_product(1, NB)
            for k in range(NH):
                pe.wait_ge(out_added[k], NB)
                out_product(k, NB)
            pe.wait_ge(zT_lo_s[0], NB)
            zT(1, NB)
            for k in range(NH, USES):
                pe.wait_ge(out_added[k], NB)
                out_product(k, NB)


INPUTS = ["x", "ctx_4096", "g_xattn", "g_ffn", "L0_xattn_Wt", "L0_xattn_Wp", "L0_xattn_Wg", "L0_xattn_Wz",
          "L0_xattn_gn_w", "L0_xattn_gn_b", "L0_ffn_A_w", "L0_ffn_B_w", "L0_ffn_Wq_w", "L0_ffn_keys"]


def kernel(**inputs):
    import numpy as np
    import concourse.bacc as bacc
    from concourse.bass_utils import run_bass_kernel_spmd

    nc = bacc.Bacc("TRN2", target_bir_lowering=False, num_devices=1)
    arrays, views = {}, []
    for name in INPUTS:
        a = np.ascontiguousarray(inputs[name])
        arrays[f"in_{name}"] = a
        views.append(nc.dram_tensor(f"in_{name}", a.shape, mybir.dt.from_np(a.dtype), kind="ExternalInput").ap())
    shape = inputs["x"].shape
    out = nc.dram_tensor("out_block", shape, mybir.dt.float32, kind="ExternalOutput").ap()
    flamingo_block(nc, *views, out)
    result = run_bass_kernel_spmd(nc, [arrays], core_ids=[0])
    return result.results[0]["out_block"]
```

```python
import concourse.bass as bass
from concourse import mybir
from contextlib import ExitStack


def flamingo_block(nc, x, ctx, g_xattn, g_ffn, Wt, Wp, Wg, Wz, gn_w, gn_b, A_w, B_w, Wq, keys, out):
    f32 = mybir.dt.float32
    f32r = mybir.dt.float32r
    ALU = mybir.AluOpType
    ACT = mybir.ActivationFunctionType

    NB, C, D = x.shape
    P = 128
    T = C // P
    HALF = 512
    NH = D // HALF
    GROUP = Wz.shape[1]
    GPT = P // GROUP
    NN = A_w.shape[0]
    NE, RD = keys.shape
    RANK = NN // NE
    KD = D // P
    KN = NN // P
    ZC = NN + NE
    ZH = ZC // 2
    E0 = ZH // RANK
    E1 = NE - E0
    EPS = 1e-5
    FFN_SCALE = 32 / 16
    TAKEN = -3.0e38
    USES = T * NH

    x_v = x.rearrange("b (t p) d -> b p t d", p=P)
    c_v = ctx.rearrange("b (t p) d -> b p t d", p=P)
    o_v = out.rearrange("b (t p) d -> b t p d", p=P)
    a_v = A_w.rearrange("(s p) d -> s p d", p=P)
    b_v = B_w.rearrange("(s t p) n -> s p t n", p=P, t=2)

    def sample(view, b):
        if isinstance(b, int):
            return view[b]
        return view[bass.ds(b, 1)].rearrange("a p t d -> (a p) t d")

    def tile_of(view, b, t):
        if isinstance(b, int):
            return view[b, t]
        return view[bass.ds(b, 1), t].rearrange("a p d -> (a p) d")

    with ExitStack() as stack:
        def sb(name, shape, dt=f32):
            return stack.enter_context(nc.sbuf_tensor(name, shape, dt))

        def sem(name):
            return stack.enter_context(nc.semaphore(name))

        def sems(name, n):
            return [sem(f"{name}{i}") for i in range(n)]

        A_hi, A_lo = sb("A_hi", [P, KD, ZC], f32r), sb("A_lo", [P, KD, ZC], f32r)
        B_hi, B_lo = sb("B_hi", [P, KN, D], f32r), sb("B_lo", [P, KN, D], f32r)
        Wp_hi, Wp_lo = sb("Wp_hi", [P, T, C], f32r), sb("Wp_lo", [P, T, C], f32r)
        Wg_hi, Wg_lo = sb("Wg_hi", [P, T, C], f32r), sb("Wg_lo", [P, T, C], f32r)
        Wu_hi, Wu_lo = sb("Wu_hi", [P, T, C], f32r), sb("Wu_lo", [P, T, C], f32r)
        x_sb, c_sb = sb("x_sb", [P, T, D]), sb("c_sb", [P, T, D])
        c_hi, c_lo = sb("c_hi", [P, T, D], f32r), sb("c_lo", [P, T, D], f32r)
        q_hi, q_lo = sb("q_hi", [P, T, D], f32r), sb("q_lo", [P, T, D], f32r)
        ln_sb = sb("ln_sb", [P, T, D])
        uw_sb = sb("uw_sb", [P, T, D])
        xt_sb = sb("xt_sb", [P, T, D])
        res_sb = sb("res_sb", [P, T, D])
        o_sb = sb("o_sb", [P, T, D])
        g_sb = sb("g_sb", [P, 2, HALF])
        hT_hi, hT_lo = sb("hT_hi", [P, T, KD * P], f32r), sb("hT_lo", [P, T, KD * P], f32r)
        zg_sb = sb("zg_sb", [P, T, NN])
        zT_hi, zT_lo = sb("zT_hi", [P, T, KN * P], f32r), sb("zT_lo", [P, T, KN * P], f32r)
        stage = sb("stage", [P, D])
        ident, group_mean = sb("ident", [P, P]), sb("group_mean", [P, P])
        minus_half = sb("minus_half", [P, T])
        gates, tg, tg2 = sb("gates", [P, 2]), sb("tg", [P, 2]), sb("tg2", [P, 1])
        gnw, gnb = sb("gnw", [P, T]), sb("gnb", [P, T])
        gnw_t, gnb_t = sb("gnw_t", [P, T]), sb("gnb_t", [P, T])
        x_st, x_mv = sb("x_st", [P, T, NH * 6]), sb("x_mv", [P, T, 2])
        x_ve, x_rs = sb("x_ve", [P, T]), sb("x_rs", [P, T])
        u_st, u_mv = sb("u_st", [P, T, NH * 6]), sb("u_mv", [P, T, 2])
        w_st, w_mv = sb("w_st", [P, T, NH * 6]), sb("w_mv", [P, T, 2])
        w_ve, w_rs = sb("w_ve", [P, T]), sb("w_rs", [P, T])
        g_mean, u_dev = sb("g_mean", [P, T]), sb("u_dev", [P, T])
        att_half, att_var = sb("att_half", [P, T]), sb("att_var", [P, 2 * T])
        va, att, a2 = sb("va", [P, 2 * T]), sb("att", [P, T]), sb("a2", [P, T])
        y_ve, y_rs = sb("y_ve", [P, T]), sb("y_rs", [P, T])
        slope, shift = sb("slope", [P, T]), sb("shift", [P, T])
        sc, sc1, sc2 = sb("sc", [P, NE]), sb("sc1", [P, NE]), sb("sc2", [P, NE])
        top_a, top_b, neg_max = sb("top_a", [P, 8]), sb("top_b", [P, 8]), sb("neg_max", [P, 1])
        ex, eg = sb("ex", [P, NE]), sb("eg", [P, NE])
        g_sum, g_rec = sb("g_sum", [P, 1]), sb("g_rec", [P, 1])

        half = T * C
        wp_nat = o_sb[:, 0, 0:half].rearrange("p (t c) -> p t c", t=T)
        wg_nat = o_sb[:, 0, half:2 * half].rearrange("p (t c) -> p t c", t=T)
        wt_nat = o_sb[:, 1, 0:half].rearrange("p (t c) -> p t c", t=T)
        wz_nat = o_sb[:, 1, half:half + T * P].rearrange("p (t m) -> p t m", t=T)
        wz_in_rows = o_sb[:, 1, half + T * P:half + T * P + T * GROUP].rearrange("p (t i) -> p t i", t=T)
        wq_nat = zg_sb[0:RD, :, :].rearrange("r t n -> r (t n)")
        keys_nat = g_sb[0:NE, 0, 0:RD]
        wzT = g_sb[:, 1, 0:T * P].rearrange("p (t o) -> p t o", t=T)
        keysT = g_sb[0:RD, 1, T * P:T * P + NE]
        lots = [stage[:, :], res_sb[:, 0, :], res_sb[:, 1, :]]
        N_LOTS = KN + KD // 2

        z_ps = [stack.enter_context(nc.psum_tensor(f"z_ps{i}", [P, HALF], f32)) for i in range(2)]
        t_ps = [stack.enter_context(nc.psum_tensor(f"t_ps{i}", [P, HALF], f32)) for i in range(2)]
        w_ps = [stack.enter_context(nc.psum_tensor(f"w_ps{i}", [P, HALF], f32)) for i in range(4)]

        x_in, c_in, gates_in, wz_in, wt_in = sem("x_in"), sem("c_in"), sem("gates_in"), sem("wz_in"), sem("wt_in")
        wp_in, wg_in, keys_in, wq_in, gn_in = sem("wp_in"), sem("wg_in"), sem("keys_in"), sem("wq_in"), sem("gn_in")
        lot_in = sems("lot_in", N_LOTS)
        o_free = sems("o_free", T)
        pool_set, consts, wz_blocks, tanh_done, c_lo_first = (
            sem("pool_set"), sem("consts"), sem("wz_blocks"), sem("tanh_done"), sem("c_lo_first"))
        prep_done, prep_hi, prep_lo = sem("prep_done"), sem("prep_hi"), sem("prep_lo")
        x_var, x_rstd, xt_done, q_done, q_hi_s, q_lo_s = (
            sem("x_var"), sem("x_rstd"), sem("xt_done"), sems("q_done", T), sems("q_hi_s", T), sem("q_lo_s"))
        c_hi_s, c_lo_s = sems("c_hi_s", T), sem("c_lo_s")
        u_done, u_copied = sems("u_done", USES), sems("u_copied", USES)
        g_done, g_copied = sems("g_done", USES), sems("g_copied", USES)
        p_done, p_reduced = sems("p_done", USES), sems("p_reduced", USES)
        u_stats, mean_sum, mean_read = sem("u_stats"), sem("mean_sum"), sem("mean_read")
        va_sum, va_read, y_var, y_rstd = sem("va_sum"), sem("va_read"), sem("y_var"), sem("y_rstd")
        w_var, w_rstd, h_done = sems("w_var", T), sems("w_rstd", T), sems("h_done", T)
        hT_done, hT_hi_s, hT_lo_s = sems("hT_done", 2 * T), sems("hT_hi_s", 2 * T), sems("hT_lo_s", 2 * T)
        res_done = sem("res_done")
        z_done, max_done, exp_done, zg_done = (
            sems("z_done", T), sems("max_done", T), sems("exp_done", T), sems("zg_done", T))
        zT_done, zT_hi_s, zT_lo_s = sems("zT_done", T), sems("zT_hi_s", T), sems("zT_lo_s", T)
        out_done, out_added = sems("out_done", USES), sems("out_added", USES)
        dve_step = sem("dve_step")

        stack.enter_context(nc.allow_non_contiguous_dma(reason="norm weights and gates: a few hundred bytes"))
        block = stack.enter_context(nc.Block())

        SMALL = ["wz", "keys", "wu", "wg", "wp", "router"]
        A_GROUPS = [("a", n, g) for n in range(KN) for g in range(KD // 4)]
        B_GROUPS = [("b", o, 0) for o in range(KD)]
        n_small, n_a, n_b = len(SMALL), len(A_GROUPS), len(B_GROUPS)
        n_first = SMALL.index("wg")
        LATE_B = 2
        PREP = [(s, 0, 0) for s in SMALL] + A_GROUPS + B_GROUPS
        LOT_DONE = [n_small + 2 * j + 2 for j in range(N_LOTS)]

        def b_groups_at(k, i=None):
            at = n_small + n_a + 2 * k
            return [n for j, n in enumerate((at, at + 1)) if n < len(PREP) - LATE_B and i in (None, j)]

        def prep_dest(n):
            kind, i, g = PREP[n]
            ps = t_ps[n % 2]
            whole = ps[:, 0:half].rearrange("p (t c) -> p t c", t=T)
            if kind == "wp":
                return whole, Wp_hi[:, :, :], Wp_lo[:, :, :]
            if kind == "wg":
                return whole, Wg_hi[:, :, :], Wg_lo[:, :, :]
            if kind == "wu":
                return whole, Wu_hi[:, :, :], Wu_lo[:, :, :]
            if kind == "wz":
                return ps[:, 0:T * P].rearrange("p (t o) -> p t o", t=T), wzT, None
            if kind == "keys":
                return ps[0:RD, 0:NE], keysT, None
            if kind == "router":
                cols = slice(NN, NN + NE)
                return ps[:, :].rearrange("p (k e) -> p k e", k=KD), A_hi[:, :, cols], A_lo[:, :, cols]
            four = ps[:, :].rearrange("p (k n) -> p k n", k=4)
            if kind == "a":
                at = (slice(None), slice(4 * g, 4 * g + 4), slice(i * P, i * P + P))
                return four, A_hi[at], A_lo[at]
            at = (slice(None), slice(0, KN), slice(i * P, i * P + P))
            return four, B_hi[at], B_lo[at]

        @block.sync
        def _(sp):
            sp.dma_start(wz_in_rows, Wz.rearrange("(t p) i -> p t i", p=P)).then_inc(wz_in, 16)
            sp.dma_start(wt_nat, Wt.rearrange("(t p) c -> p t c", p=P)).then_inc(wt_in, 16)
            sp.dma_start(c_sb[:, :, :], sample(c_v, 0)).then_inc(c_in, 16)
            sp.dma_start(wg_nat, Wg.rearrange("(t p) c -> p t c", p=P)).then_inc(wg_in, 16)
            sp.dma_start(wp_nat, Wp.rearrange("(t p) c -> p t c", p=P)).then_inc(wp_in, 16)
            sp.dma_start(x_sb[:, :, :], sample(x_v, 0)).then_inc(x_in, 16)

            def load_lot(j):
                place = lots[j % len(lots)]
                if j >= len(lots):
                    sp.wait_ge(prep_done, LOT_DONE[j - len(lots)])
                if j < KN:
                    sp.dma_start(place, a_v[j]).then_inc(lot_in[j], 16)
                else:
                    sp.dma_start(place.rearrange("p (t n) -> p t n", t=2), b_v[j - KN]).then_inc(lot_in[j], 16)

            for j in range(len(lots)):
                load_lot(j)
            for j in range(len(lots), N_LOTS):
                load_lot(j)

            def load(b, n_prev):
                sp.wait_ge(xt_done, n_prev)
                sp.wait_ge(c_lo_s, n_prev)
                sp.dma_start(x_sb[:, :, :], sample(x_v, b)).then_inc(x_in, 16)
                sp.dma_start(c_sb[:, :, :], sample(c_v, b)).then_inc(c_in, 16)

            def store(b, n):
                for t in range(T):
                    sp.wait_ge(out_added[NH * t + NH - 1], n + 1)
                    sp.dma_start(tile_of(o_v, b, t), o_sb[:, t, :]).then_inc(o_free[t], 16)

            load(1, 1)
            with sp.Fori(0, NB - 2) as b:
                load(b + 2, sp.snap(b + 2))
                store(b, b + 1)
            for b in range(NB - 2, NB):
                store(b, b + 1)
            for t in range(T):
                sp.wait_ge(o_free[t], 16 * (NB + 1))

        @block.gpsimd
        def _(pool):
            pool.memset(ident[:, :], 0.0).then_inc(pool_set, 1)
            pool.memset(minus_half[:, :], -0.5).then_inc(pool_set, 1)
            pool.wait_ge(pool_set, 2)
            pool.affine_select(out=ident[:, :], in_=ident[:, :], compare_op=ALU.not_equal, fill=1.0,
                               base=0, pattern=[[-1, P]], channel_multiplier=1).then_inc(consts, 1)

            def attention(n, prev):
                for t in range(1 if prev is None else 0, T):
                    pool.wait_ge(c_hi_s[t], n)
                    if prev is not None:
                        pool.wait_ge(p_done[USES - 1], prev)
                    last = pool.tensor_tensor(c_lo[:, t, :], c_sb[:, t, :], c_hi[:, t, :].bitcast(f32),
                                              ALU.subtract)
                last.then_inc(c_lo_s, 1)
                pool.wait_ge(x_var, n)
                pool.tensor_tensor(x_rs[:, :], x_ve[:, :], minus_half[:, :], ALU.pow).then_inc(x_rstd, 1)
                for t in range(T):
                    pool.wait_ge(q_hi_s[t], n)
                    last = pool.tensor_tensor(q_lo[:, t, :], ln_sb[:, t, :], q_hi[:, t, :].bitcast(f32),
                                              ALU.subtract)
                last.then_inc(q_lo_s, 1)
                pool.wait_ge(y_var, n)
                pool.tensor_tensor(y_rs[:, :], y_ve[:, :], minus_half[:, :], ALU.pow).then_inc(y_rstd, 1)
                for t in range(T):
                    pool.wait_ge(w_var[t], n)
                    pool.tensor_tensor(w_rs[:, t:t + 1], w_ve[:, t:t + 1], minus_half[:, t:t + 1],
                                       ALU.pow).then_inc(w_rstd[t], 1)

            attention(1, None)
            with pool.Fori(0, NB - 1) as b:
                attention(pool.snap(b + 2), pool.snap(b + 1))

        @block.scalar
        def _(act):
            act.dma_start(keys_nat, keys).then_inc(keys_in, 16)
            act.dma_start(wq_nat, Wq).then_inc(wq_in, 16)
            act.dma_start(gates[:, 0:1], g_xattn.partition_broadcast(P)).then_inc(gates_in, 16)
            act.dma_start(gates[:, 1:2], g_ffn.partition_broadcast(P)).then_inc(gates_in, 16)
            act.dma_start(gnw[:, :], gn_w.rearrange("(t p) -> p t", p=P)).then_inc(gn_in, 16)
            act.dma_start(gnb[:, :], gn_b.rearrange("(t p) -> p t", p=P)).then_inc(gn_in, 16)

            def prep(n):
                src, hi, lo = prep_dest(n)
                act.wait_ge(prep_done, n + 1)
                act.activation(hi, src, ACT.Copy).then_inc(prep_hi, 1)

            def ctx_hi(n, prev):
                act.wait_ge(c_in, 16 if prev is None else act_c_in)
                if prev is not None:
                    act.wait_ge(p_done[USES - 1], prev)
                for t in range(T):
                    act.activation(c_hi[:, t, :], c_sb[:, t, :], ACT.Copy).then_inc(c_hi_s[t], 1)

            def query_hi(n):
                for t in range(T):
                    act.wait_ge(q_done[t], n)
                    act.activation(q_hi[:, t, :], ln_sb[:, t, :], ACT.Copy).then_inc(q_hi_s[t], 1)

            def residual(n):
                act.wait_ge(h_done[T - 1], n)
                act.wait_ge(out_added[USES - 1], n)
                for t in range(T):
                    last = act.activation(res_sb[:, t, :], uw_sb[:, t, :], ACT.Identity, bias=shift[:, t:t + 1])
                last.then_inc(res_done, 1)

            def u_copy(k, n):
                t, h = divmod(k, NH)
                act.wait_ge(u_done[k], n)
                act.activation(uw_sb[:, t, h * HALF:(h + 1) * HALF], w_ps[k][:, :], ACT.Copy).then_inc(u_copied[k], 1)

            def g_copy(k, n):
                act.wait_ge(g_done[k], n)
                if k >= 2:
                    act.wait_ge(p_reduced[k - 2], n)
                act.activation(g_sb[:, k % 2, :], w_ps[2 * (k % 2)][:, :], ACT.Copy).then_inc(g_copied[k], 1)

            def hT_high(t, n):
                for g in range(2):
                    k = 2 * t + g
                    act.wait_ge(hT_done[k], n)
                    act.activation(hT_hi[:, t, g * HALF:(g + 1) * HALF], t_ps[g][:, :], ACT.Copy)\
                       .then_inc(hT_hi_s[k], 1)

            def zT_high(t, n):
                act.wait_ge(zT_done[t], n)
                act.activation(zT_hi[:, t, :], t_ps[0][:, :], ACT.Copy).then_inc(zT_hi_s[t], 1)

            def exps(t, n):
                act.wait_ge(max_done[t], n)
                act.activation(ex[:, :], sc[:, :], ACT.Exp, bias=neg_max[:, 0:1]).then_inc(exp_done[t], 1)

            for n in range(n_first):
                prep(n)
            ctx_hi(1, None)
            for n in range(n_first, n_small):
                prep(n)
            act.wait_ge(gates_in, 32)
            act.activation(tg[:, :], gates[:, :], ACT.Tanh).then_inc(tanh_done, 1)
            for k in range(USES):
                u_copy(k, 1)
                prep(n_small + 2 * k)
                prep(n_small + 2 * k + 1)
                if k == 1:
                    query_hi(1)
            for k in range(USES):
                g_copy(k, 1)
                for n in b_groups_at(k):
                    prep(n)
            for n in range(len(PREP) - LATE_B, len(PREP)):
                prep(n)
            hT_high(0, 1)

            def ffn_and_next(n, m):
                ctx_hi(m, n)
                residual(n)
                hT_high(1, n)
                exps(0, n)
                act.wait_ge(res_done, n)
                for k in range(USES):
                    u_copy(k, m)
                zT_high(0, n)
                query_hi(m)
                exps(1, n)
                for k in range(USES):
                    g_copy(k, m)
                    if k == 2:
                        zT_high(1, n)
                hT_high(0, m)

            with act.Fori(0, NB - 1) as b:
                act_c_in = act.snap(16 * b + 32)
                ffn_and_next(act.snap(b + 1), act.snap(b + 2))
            residual(NB)
            hT_high(1, NB)
            exps(0, NB)
            zT_high(0, NB)
            exps(1, NB)
            zT_high(1, NB)

        @block.vector
        def _(dve):
            steps = [0]

            def step(instruction):
                instruction.then_inc(dve_step, 1)
                steps[0] += 1

            def settle():
                dve.wait_ge(dve_step, steps[0])

            def fresh_steps():
                settle()
                dve.sem_clear(dve_step)
                steps[0] = 0

            def prep(n):
                src, hi, lo = prep_dest(n)
                dve.wait_ge(prep_hi, n + 1)
                if lo is None:
                    dve.engine_nop().then_inc(prep_lo, 1)
                    return
                dve.tensor_tensor(lo, src, hi.bitcast(f32), ALU.subtract).then_inc(prep_lo, 1)

            def x_stats(n, n_dma):
                dve.wait_ge(x_in, n_dma)
                for t in range(T):
                    for h in range(NH):
                        step(dve.bn_stats(x_st[:, t, 6 * h:6 * h + 6], x_sb[:, t, h * HALF:(h + 1) * HALF]))
                settle()
                for t in range(T):
                    step(dve.bn_aggr(x_mv[:, t, :], x_st[:, t, :]))
                settle()
                dve.tensor_scalar(x_ve[:, :], x_mv[:, :, 1], EPS, None, ALU.add).then_inc(x_var, 1)

            def x_plus_ctx(n, n_dma):
                dve.wait_ge(c_in, n_dma)
                for t in range(T):
                    last = dve.scalar_tensor_tensor(xt_sb[:, t, :], c_sb[:, t, :], tg[:, 0:1], x_sb[:, t, :],
                                                    ALU.mult, ALU.add)
                last.then_inc(xt_done, 1)

            def query(n, prev):
                dve.wait_ge(x_rstd, n)
                if prev is not None:
                    dve.wait_ge(hT_done[2 * T - 1], prev)
                for t in range(T):
                    dve.tensor_scalar(ln_sb[:, t, :], x_sb[:, t, :], x_mv[:, t, 0:1], x_rs[:, t:t + 1],
                                      ALU.subtract, ALU.mult).then_inc(q_done[t], 1)

            def gate(t, n, banks=z_ps):
                dve.wait_ge(z_done[t], n)
                step(dve.tensor_copy(sc[:, :], banks[1][:, ZH - NE:ZH]))
                settle()
                step(dve.max(top_a[:, :], sc[:, :]))
                settle()
                dve.tensor_scalar(neg_max[:, :], top_a[:, 0:1], -1.0, None, ALU.mult).then_inc(max_done[t], 1)
                step(dve.match_replace(sc1[:, :], top_a[:, :], sc[:, :], TAKEN))
                settle()
                step(dve.max(top_b[:, :], sc1[:, :]))
                settle()
                step(dve.match_replace(sc2[:, :], top_b[:, :], sc1[:, :], TAKEN))
                settle()
                dve.wait_ge(exp_done[t], n)
                step(dve.scalar_tensor_tensor(eg[:, :], sc2[:, :], TAKEN, ex[:, :], ALU.is_equal, ALU.mult,
                                              accum_out=g_sum[:, :]))
                settle()
                step(dve.reciprocal(g_rec[:, :], g_sum[:, :]))
                settle()
                for i, (e, k) in enumerate(((0, E0), (E0, E1))):
                    last = dve.scalar_tensor_tensor(
                        zg_sb[:, t, e * RANK:(e + k) * RANK].rearrange("p (e r) -> p e r", r=RANK),
                        banks[i][:, 0:k * RANK].rearrange("p (e r) -> p e r", r=RANK), g_rec[:, :],
                        eg[:, e:e + k].unsqueeze(2).to_broadcast([P, k, RANK]), ALU.mult, ALU.mult)
                last.then_inc(zg_done[t], 1)

            def hT_low(t, n):
                for g in range(2):
                    k = 2 * t + g
                    at = (slice(None), t, slice(g * HALF, (g + 1) * HALF))
                    dve.wait_ge(hT_hi_s[k], n)
                    dve.tensor_tensor(hT_lo[at], t_ps[g][:, :], hT_hi[at].bitcast(f32), ALU.subtract)\
                       .then_inc(hT_lo_s[k], 1)

            def zT_low(t, n):
                dve.wait_ge(zT_hi_s[t], n)
                dve.tensor_tensor(zT_lo[:, t, :], t_ps[0][:, :], zT_hi[:, t, :].bitcast(f32), ALU.subtract)\
                   .then_inc(zT_lo_s[t], 1)

            def u_statistics(n):
                for k in range(USES):
                    t, h = divmod(k, NH)
                    dve.wait_ge(u_copied[k], n)
                    step(dve.bn_stats(u_st[:, t, 6 * h:6 * h + 6], uw_sb[:, t, h * HALF:(h + 1) * HALF]))
                settle()
                for t in range(T):
                    last = dve.bn_aggr(u_mv[:, t, :], u_st[:, t, :])
                last.then_inc(u_stats, 1)

            def group_deviation(n):
                dve.wait_ge(mean_sum, n)
                dve.tensor_copy(g_mean[:, :], t_ps[1][:, 0:T]).then_inc(mean_read, 1)
                dve.wait_ge(mean_read, n)
                step(dve.tensor_tensor(u_dev[:, :], u_mv[:, :, 0], g_mean[:, :], ALU.subtract))
                settle()
                step(dve.tensor_tensor(a2[:, :], u_dev[:, :], u_dev[:, :], ALU.mult))
                settle()
                step(dve.tensor_tensor(att_var[:, T:2 * T], a2[:, :], u_mv[:, :, 1], ALU.add))

            def reduce_pg(k, n):
                t, h = divmod(k, NH)
                into = att_half[:, t:t + 1] if h == 0 else att_var[:, t:t + 1]
                dve.wait_ge(g_copied[k], n)
                if h > 0:
                    dve.wait_ge(p_reduced[k - 1], n)
                dve.wait_ge(p_done[k], n)
                dve.tensor_tensor_reduce(out=g_sb[:, k % 2, :], in0=w_ps[2 * (k % 2) + 1][:, :],
                                         in1=g_sb[:, k % 2, :], scale=1.0,
                                         scalar=0.0 if h == 0 else att_half[:, t:t + 1],
                                         op0=ALU.mult, op1=ALU.add, accum_out=into).then_inc(p_reduced[k], 1)

            def slopes(n, meanwhile):
                dve.wait_ge(va_sum, n)
                dve.tensor_copy(va[:, :], t_ps[1][:, 0:2 * T]).then_inc(va_read, 1)
                dve.wait_ge(va_read, n)
                step(dve.tensor_scalar(att[:, :], va[:, 0:T], float(GROUP), None, ALU.mult))
                settle()
                step(dve.tensor_tensor(a2[:, :], att[:, :], att[:, :], ALU.mult))
                settle()
                step(dve.tensor_tensor(a2[:, :], a2[:, :], va[:, T:2 * T], ALU.mult))
                step(dve.tensor_tensor(att[:, :], att[:, :], gnw_t[:, :], ALU.mult))
                settle()
                dve.tensor_scalar(y_ve[:, :], a2[:, :], EPS, None, ALU.add).then_inc(y_var, 1)
                meanwhile()
                dve.wait_ge(y_rstd, n)
                step(dve.tensor_tensor(slope[:, :], att[:, :], y_rs[:, :], ALU.mult))
                settle()

            def w_tile(t, meanwhile=None):
                step(dve.scalar_tensor_tensor(uw_sb[:, t, :], uw_sb[:, t, :], slope[:, t:t + 1], xt_sb[:, t, :],
                                              ALU.mult, ALU.add))
                settle()
                for h in range(NH):
                    step(dve.bn_stats(w_st[:, t, 6 * h:6 * h + 6], uw_sb[:, t, h * HALF:(h + 1) * HALF]))
                if meanwhile:
                    meanwhile()
                settle()
                step(dve.bn_aggr(w_mv[:, t, :], w_st[:, t, :]))
                settle()
                dve.tensor_scalar(w_ve[:, t:t + 1], w_mv[:, t, 1:2], EPS, None, ALU.add).then_inc(w_var[t], 1)

            def shifts():
                step(dve.tensor_tensor(shift[:, :], g_mean[:, :], slope[:, :], ALU.mult))
                settle()
                step(dve.tensor_tensor(shift[:, :], gnb_t[:, :], shift[:, :], ALU.subtract))

            def h_tile(t, n):
                dve.wait_ge(w_rstd[t], n)
                dve.wait_ge(q_lo_s, n)
                dve.tensor_scalar(ln_sb[:, t, :], uw_sb[:, t, :], w_mv[:, t, 0:1], w_rs[:, t:t + 1],
                                  ALU.subtract, ALU.mult).then_inc(h_done[t], 1)

            def finish_attention(n, add=lambda k: None):
                slopes(n, lambda: add(0))
                w_tile(0)
                shifts()
                add(1)
                h_tile(0, n)
                w_tile(1, lambda: hT_low(0, n))
                add(2)
                h_tile(1, n)
                add(3)

            def add_out(k, n, n_dma):
                t, h = divmod(k, NH)
                cols = slice(h * HALF, (h + 1) * HALF)
                if h == 0:
                    dve.wait_ge(o_free[t], n_dma)
                if k == 0:
                    dve.wait_ge(res_done, n)
                dve.wait_ge(out_done[k], n)
                dve.scalar_tensor_tensor(o_sb[:, t, cols], w_ps[k][:, :], tg2[:, 0:1], res_sb[:, t, cols],
                                         ALU.mult, ALU.add).then_inc(out_added[k], 1)

            step(dve.memset(wz_nat, 0.0))
            step(dve.memset(group_mean[:, :], 0.0))
            settle()
            for g in range(GPT):
                rows = slice(g * GROUP, g * GROUP + GROUP)
                dve.memset(group_mean[rows, rows], 1.0 / GROUP).then_inc(consts, 1)
            dve.wait_ge(wz_in, 16)
            for g in range(GPT):
                rows = slice(g * GROUP, g * GROUP + GROUP)
                last = dve.tensor_copy(wz_nat[rows, :, rows], wz_in_rows[rows, :, :])
            last.then_inc(wz_blocks, 1)
            for n in range(n_first):
                prep(n)
            dve.wait_ge(c_hi_s[0], 1)
            dve.tensor_tensor(c_lo[:, 0, :], c_sb[:, 0, :], c_hi[:, 0, :].bitcast(f32), ALU.subtract)\
               .then_inc(c_lo_first, 1)
            for n in range(n_first, n_small):
                prep(n)
            x_stats(1, 16)
            for k in range(USES):
                prep(n_small + 2 * k)
                prep(n_small + 2 * k + 1)
                if k == 0:
                    query(1, None)
            u_statistics(1)
            dve.wait_ge(gn_in, 32)
            dve.wait_ge(tanh_done, 1)
            step(dve.tensor_scalar(gnw_t[:, :], gnw[:, :], tg[:, 0:1], None, ALU.mult))
            step(dve.tensor_scalar(gnb_t[:, :], gnb[:, :], tg[:, 0:1], None, ALU.mult))
            step(dve.tensor_scalar(tg2[:, :], tg[:, 1:2], FFN_SCALE, None, ALU.mult))
            for k in range(USES):
                for n in b_groups_at(k, 0):
                    prep(n)
                if k == 2:
                    group_deviation(1)
                reduce_pg(k, 1)
                for n in b_groups_at(k, 1):
                    prep(n)
                if k == 1:
                    x_plus_ctx(1, 16)
            finish_attention(1, lambda k: prep(len(PREP) - LATE_B + k) if k < LATE_B else None)
            fresh_steps()

            def ffn_and_next(n, m, n_dma, m_dma):
                x_stats(m, m_dma)
                hT_low(1, n)
                query(m, n)
                gate(0, n)
                x_plus_ctx(m, m_dma)
                u_statistics(m)
                zT_low(0, n)
                gate(1, n)
                group_deviation(m)
                for k in range(USES):
                    reduce_pg(k, m)
                    if k == 1:
                        zT_low(1, n)
                finish_attention(m, lambda k: add_out(k, n, n_dma))
                fresh_steps()

            with dve.Fori(0, NB - 1) as b:
                ffn_and_next(dve.snap(b + 1), dve.snap(b + 2), dve.snap(16 * b + 16), dve.snap(16 * b + 32))
            hT_low(1, NB)
            gate(0, NB)
            zT_low(0, NB)
            gate(1, NB, w_ps[NH:USES])
            for k in range(NH):
                add_out(k, NB, 16 * NB)
            zT_low(1, NB)
            for k in range(NH, USES):
                add_out(k, NB, 16 * NB)

        @block.tensor
        def _(pe):
            def prep(n):
                kind, i, g = PREP[n]
                ps = t_ps[n % 2]
                if n >= 2:
                    pe.wait_ge(prep_lo, n - 1)
                if kind in ("wp", "wg"):
                    nat, arrived = (wp_nat, wp_in) if kind == "wp" else (wg_nat, wg_in)
                    pe.wait_ge(arrived, 16)
                    for o in range(T):
                        for c in range(T):
                            last = pe.transpose(ps[:, c * C + o * P:c * C + o * P + P],
                                                nat[:, o, c * P:c * P + P], ident[:, :])
                elif kind == "wz":
                    pe.wait_ge(wz_blocks, 1)
                    for o in range(T):
                        last = pe.transpose(ps[:, o * P:o * P + P], wz_nat[:, o, :], ident[:, :])
                elif kind == "wu":
                    pe.wait_ge(wt_in, 16)
                    pe.wait_ge(prep_hi, SMALL.index("wz") + 1)
                    for o in range(T):
                        for c in range(T):
                            last = pe.matmul(ps[:, c * C + o * P:c * C + o * P + P],
                                             wt_nat[:, o, c * P:c * P + P], wzT[:, o, :], start=True, stop=True)
                elif kind == "keys":
                    pe.wait_ge(keys_in, 16)
                    last = pe.transpose(ps[0:RD, 0:NE], keys_nat, ident[0:NE, 0:NE])
                elif kind == "router":
                    pe.wait_ge(wq_in, 16)
                    pe.wait_ge(prep_hi, SMALL.index("keys") + 1)
                    for k in range(KD):
                        last = pe.matmul(ps[:, k * NE:k * NE + NE], wq_nat[:, k * P:k * P + P], keysT,
                                         start=True, stop=True)
                elif kind == "a":
                    pe.wait_ge(lot_in[i], 16)
                    for k in range(4):
                        d = (4 * g + k) * P
                        last = pe.transpose(ps[:, k * P:k * P + P], lots[i % len(lots)][:, d:d + P], ident[:, :])
                else:
                    j = KN + i // 2
                    pe.wait_ge(lot_in[j], 16)
                    for k in range(KN):
                        at = (i % 2) * NN + k * P
                        last = pe.transpose(ps[:, k * P:k * P + P], lots[j % len(lots)][:, at:at + P], ident[:, :])
                last.then_inc(prep_done, 1)

            def product(ps, w_hi, w_lo, v_hi, v_lo, k, ins):
                t, h = divmod(k, NH)
                rows, cols = slice(t * P, t * P + P), slice(h * HALF, (h + 1) * HALF)
                passes = [(w, v, c) for c in range(T) for w, v in ((w_hi, v_hi), (w_hi, v_lo), (w_lo, v_hi))]
                for i, (w, v, c) in enumerate(passes):
                    last = pe.matmul(ps, w[:, c, rows], v[:, c, cols], start=(i == 0), stop=(i == len(passes) - 1))
                last.then_inc(ins, 1)

            def u_product(n, between=None):
                pe.wait_ge(c_lo_s, n)
                for k in range(USES):
                    product(w_ps[k][:, :], Wu_hi, Wu_lo, c_hi, c_lo, k, u_done[k])
                    if between:
                        between(k)

            def pg_products(n, between):
                for k in range(USES):
                    first = 2 * (k % 2)
                    pe.wait_ge(u_copied[first] if k < 2 else g_copied[k - 2], n)
                    product(w_ps[first][:, :], Wg_hi, Wg_lo, c_hi, c_lo, k, g_done[k])
                    between(k, 0)
                    if k == 0:
                        pe.wait_ge(q_lo_s, n)
                    pe.wait_ge(u_copied[first + 1] if k < 2 else p_reduced[k - 2], n)
                    product(w_ps[first + 1][:, :], Wp_hi, Wp_lo, q_hi, q_lo, k, p_done[k])
                    between(k, 1)

            def group_means(n):
                pe.wait_ge(u_stats, n)
                pe.matmul(t_ps[1][:, 0:T], group_mean[:, :], u_mv[:, :, 0], start=True, stop=True)\
                  .then_inc(mean_sum, 1)

            def group_att_var(n):
                pe.wait_ge(mean_read, n)
                pe.wait_ge(p_reduced[USES - 1], n)
                pe.matmul(t_ps[1][:, 0:2 * T], group_mean[:, :], att_var[:, :], start=True, stop=True)\
                  .then_inc(va_sum, 1)

            def hT(t, n):
                pe.wait_ge(h_done[t], n)
                for g in range(2):
                    for k in range(4):
                        d = (4 * g + k) * P
                        last = pe.transpose(t_ps[g][:, k * P:k * P + P], ln_sb[:, t, d:d + P], ident[:, :])
                    last.then_inc(hT_done[2 * t + g], 1)
                    if g == 0:
                        pe.wait_ge(va_read if t == 0 else hT_lo_s[1], n)

            def z_product(t, n, middle=None, banks=z_ps):
                for k in range(KD):
                    if k % 4 == 0:
                        pe.wait_ge(hT_lo_s[2 * t + k // 4], n)
                    row = slice(k * P, k * P + P)
                    for h, w in ((hT_hi, A_hi), (hT_hi, A_lo), (hT_lo, A_hi)):
                        for i in range(2):
                            last = pe.matmul(banks[i][:, 0:ZH], h[:, t, row], w[:, k, i * ZH:(i + 1) * ZH],
                                             start=(k == 0 and h is hT_hi and w is A_hi),
                                             stop=(k == KD - 1 and h is hT_lo))
                    if k == 3 and middle:
                        middle()
                last.then_inc(z_done[t], 1)

            def zT(t, n):
                pe.wait_ge(zg_done[t], n)
                for k in range(KN):
                    last = pe.transpose(t_ps[0][:, k * P:k * P + P], zg_sb[:, t, k * P:k * P + P], ident[:, :])
                last.then_inc(zT_done[t], 1)

            def out_product(k, n, middle=None):
                t, h = divmod(k, NH)
                cols = slice(h * HALF, (h + 1) * HALF)
                pe.wait_ge(zT_lo_s[t], n)
                for j in range(KN):
                    row = slice(j * P, j * P + P)
                    for z, w in ((zT_hi, B_hi), (zT_hi, B_lo), (zT_lo, B_hi)):
                        last = pe.matmul(w_ps[k][:, :], z[:, t, row], w[:, j, cols],
                                         start=(j == 0 and z is zT_hi and w is B_hi),
                                         stop=(j == KN - 1 and z is zT_lo))
                    if j == KN // 2 - 1 and middle:
                        middle()
                last.then_inc(out_done[k], 1)

            for t in range(T):
                pe.sem_inc(o_free[t], 16)
            for k in range(USES):
                pe.sem_inc(out_added[k], 1)
            pe.wait_ge(consts, 1 + GPT)
            for n in range(n_small):
                prep(n)

            def prep_a(k):
                prep(n_small + 2 * k)
                prep(n_small + 2 * k + 1)

            pe.wait_ge(c_lo_first, 1)
            u_product(1, prep_a)

            def prep_b(k, i):
                if (k, i) == (2, 0):
                    pe.wait_ge(prep_lo, b_groups_at(1)[-1] + 1)
                    group_means(1)
                if (k, i) == (2, 1):
                    pe.wait_ge(mean_read, 1)
                for n in b_groups_at(k, i):
                    prep(n)

            pg_products(1, prep_b)
            pe.wait_ge(prep_lo, len(PREP) - LATE_B)
            group_att_var(1)
            for n in range(len(PREP) - LATE_B, len(PREP)):
                if n % 2 == 1:
                    pe.wait_ge(va_read, 1)
                prep(n)
            pe.wait_ge(prep_lo, len(PREP))
            hT(0, 1)

            def ffn_and_next(n, m):
                def second_tile():
                    pe.wait_ge(hT_lo_s[0], n)
                    hT(1, n)

                z_product(0, n, second_tile)
                u_product_next(n, m)
                pe.wait_ge(hT_lo_s[2], n)
                zT(0, n)
                pe.wait_ge(zg_done[0], n)
                z_product(1, n)
                pe.wait_ge(hT_lo_s[3], n)
                group_means(m)

                def between(k, i):
                    if (k, i) == (2, 0):
                        pe.wait_ge(zT_lo_s[0], n)
                        zT(1, n)

                pg_products(m, between)
                pe.wait_ge(g_copied[2], m)
                out_product(0, n, lambda: group_att_var(m))
                pe.wait_ge(p_reduced[2], m)
                out_product(1, n)
                pe.wait_ge(g_copied[3], m)
                out_product(2, n)
                pe.wait_ge(zT_lo_s[1], n)
                hT(0, m)
                pe.wait_ge(p_reduced[3], m)
                out_product(3, n)

            def u_product_next(n, m):
                pe.wait_ge(c_lo_s, m)
                for k in range(USES):
                    pe.wait_ge(out_added[k], n)
                    product(w_ps[k][:, :], Wu_hi, Wu_lo, c_hi, c_lo, k, u_done[k])

            with pe.Fori(0, NB - 1) as b:
                ffn_and_next(pe.snap(b + 1), pe.snap(b + 2))

            def last_second_tile():
                pe.wait_ge(hT_lo_s[0], NB)
                hT(1, NB)

            z_product(0, NB, last_second_tile)
            for k in range(USES):
                pe.wait_ge(out_added[k], NB)
            z_product(1, NB, banks=w_ps[NH:USES])
            pe.wait_ge(hT_lo_s[2], NB)
            zT(0, NB)
            for k in range(NH):
                out_product(k, NB)
            pe.wait_ge(zT_lo_s[0], NB)
            zT(1, NB)
            for k in range(NH, USES):
                out_product(k, NB)


INPUTS = ["x", "ctx_4096", "g_xattn", "g_ffn", "L0_xattn_Wt", "L0_xattn_Wp", "L0_xattn_Wg", "L0_xattn_Wz",
          "L0_xattn_gn_w", "L0_xattn_gn_b", "L0_ffn_A_w", "L0_ffn_B_w", "L0_ffn_Wq_w", "L0_ffn_keys"]


def kernel(**inputs):
    import numpy as np
    import concourse.bacc as bacc
    from concourse.bass_utils import run_bass_kernel_spmd

    nc = bacc.Bacc("TRN2", target_bir_lowering=False, num_devices=1)
    arrays, views = {}, []
    for name in INPUTS:
        a = np.ascontiguousarray(inputs[name])
        arrays[f"in_{name}"] = a
        views.append(nc.dram_tensor(f"in_{name}", a.shape, mybir.dt.from_np(a.dtype), kind="ExternalInput").ap())
    shape = inputs["x"].shape
    out = nc.dram_tensor("out_block", shape, mybir.dt.float32, kind="ExternalOutput").ap()
    flamingo_block(nc, *views, out)
    result = run_bass_kernel_spmd(nc, [arrays], core_ids=[0])
    return result.results[0]["out_block"]
```

```python
import concourse.bass as bass
from concourse import mybir
from contextlib import ExitStack


def flamingo_block(nc, x, ctx, g_xattn, g_ffn, Wt, Wp, Wg, Wz, gn_w, gn_b, A_w, B_w, Wq, keys, out):
    f32 = mybir.dt.float32
    f32r = mybir.dt.float32r
    ALU = mybir.AluOpType
    ACT = mybir.ActivationFunctionType

    NB, C, D = x.shape
    P = 128
    T = C // P
    HALF = 512
    NH = D // HALF
    GROUP = Wz.shape[1]
    GPT = P // GROUP
    NN = A_w.shape[0]
    NE, RD = keys.shape
    RANK = NN // NE
    KD = D // P
    KN = NN // P
    ZC = NN + NE
    ZH = ZC // 2
    E0 = ZH // RANK
    E1 = NE - E0
    EPS = 1e-5
    FFN_SCALE = 32 / 16
    TAKEN = -3.0e38
    USES = T * NH

    x_v = x.rearrange("b (t p) d -> b p t d", p=P)
    c_v = ctx.rearrange("b (t p) d -> b p t d", p=P)
    o_v = out.rearrange("b (t p) d -> b t p d", p=P)
    a_v = A_w.rearrange("(s p) d -> s p d", p=P)
    b_v = B_w.rearrange("(s t p) n -> s p t n", p=P, t=2)

    def sample(view, b):
        if isinstance(b, int):
            return view[b]
        return view[bass.ds(b, 1)].rearrange("a p t d -> (a p) t d")

    def tile_of(view, b, t):
        if isinstance(b, int):
            return view[b, t]
        return view[bass.ds(b, 1), t].rearrange("a p d -> (a p) d")

    with ExitStack() as stack:
        def sb(name, shape, dt=f32):
            return stack.enter_context(nc.sbuf_tensor(name, shape, dt))

        def sem(name):
            return stack.enter_context(nc.semaphore(name))

        def sems(name, n):
            return [sem(f"{name}{i}") for i in range(n)]

        A_hi, A_lo = sb("A_hi", [P, KD, ZC], f32r), sb("A_lo", [P, KD, ZC], f32r)
        B_hi, B_lo = sb("B_hi", [P, KN, D], f32r), sb("B_lo", [P, KN, D], f32r)
        Wp_hi, Wp_lo = sb("Wp_hi", [P, T, C], f32r), sb("Wp_lo", [P, T, C], f32r)
        Wg_hi, Wg_lo = sb("Wg_hi", [P, T, C], f32r), sb("Wg_lo", [P, T, C], f32r)
        Wu_hi, Wu_lo = sb("Wu_hi", [P, T, C], f32r), sb("Wu_lo", [P, T, C], f32r)
        x_sb, c_sb = sb("x_sb", [P, T, D]), sb("c_sb", [P, T, D])
        c_hi, c_lo = sb("c_hi", [P, T, D], f32r), sb("c_lo", [P, T, D], f32r)
        q_hi, q_lo = sb("q_hi", [P, T, D], f32r), sb("q_lo", [P, T, D], f32r)
        ln_sb = sb("ln_sb", [P, T, D])
        uw_sb = sb("uw_sb", [P, T, D])
        xt_sb = sb("xt_sb", [P, T, D])
        res_sb = sb("res_sb", [P, T, D])
        o_sb = sb("o_sb", [P, T, D])
        g_sb = sb("g_sb", [P, 2, HALF])
        hT_hi, hT_lo = sb("hT_hi", [P, T, KD * P], f32r), sb("hT_lo", [P, T, KD * P], f32r)
        zg_sb = sb("zg_sb", [P, T, NN])
        zT_hi, zT_lo = sb("zT_hi", [P, T, KN * P], f32r), sb("zT_lo", [P, T, KN * P], f32r)
        stage = sb("stage", [P, D])
        ident, group_mean = sb("ident", [P, P]), sb("group_mean", [P, P])
        minus_half = sb("minus_half", [P, T])
        gates, tg, tg2 = sb("gates", [P, 2]), sb("tg", [P, 2]), sb("tg2", [P, 1])
        gnw, gnb = sb("gnw", [P, T]), sb("gnb", [P, T])
        gnw_t, gnb_t = sb("gnw_t", [P, T]), sb("gnb_t", [P, T])
        x_st, x_mv = sb("x_st", [P, T, NH * 6]), sb("x_mv", [P, T, 2])
        x_ve, x_rs = sb("x_ve", [P, T]), sb("x_rs", [P, T])
        u_st, u_mv = sb("u_st", [P, T, NH * 6]), sb("u_mv", [P, T, 2])
        w_st, w_mv = sb("w_st", [P, T, NH * 6]), sb("w_mv", [P, T, 2])
        w_ve, w_rs = sb("w_ve", [P, T]), sb("w_rs", [P, T])
        g_mean, u_dev = sb("g_mean", [P, T]), sb("u_dev", [P, T])
        att_half, att_var = sb("att_half", [P, T]), sb("att_var", [P, 2 * T])
        va, att, a2 = sb("va", [P, 2 * T]), sb("att", [P, T]), sb("a2", [P, T])
        y_ve, y_rs = sb("y_ve", [P, T]), sb("y_rs", [P, T])
        slope, shift = sb("slope", [P, T]), sb("shift", [P, T])
        sc, sc1, sc2 = sb("sc", [P, NE]), sb("sc1", [P, NE]), sb("sc2", [P, NE])
        top_a, top_b, neg_max = sb("top_a", [P, 8]), sb("top_b", [P, 8]), sb("neg_max", [P, 1])
        ex, eg = sb("ex", [P, NE]), sb("eg", [P, NE])
        g_sum, g_rec = sb("g_sum", [P, 1]), sb("g_rec", [P, 1])

        half = T * C
        wp_nat = o_sb[:, 0, 0:half].rearrange("p (t c) -> p t c", t=T)
        wg_nat = o_sb[:, 0, half:2 * half].rearrange("p (t c) -> p t c", t=T)
        wt_nat = o_sb[:, 1, 0:half].rearrange("p (t c) -> p t c", t=T)
        wz_nat = o_sb[:, 1, half:half + T * P].rearrange("p (t m) -> p t m", t=T)
        wz_in_rows = o_sb[:, 1, half + T * P:half + T * P + T * GROUP].rearrange("p (t i) -> p t i", t=T)
        wq_nat = zg_sb[0:RD, :, :].rearrange("r t n -> r (t n)")
        keys_nat = g_sb[0:NE, 0, 0:RD]
        wzT = g_sb[:, 1, 0:T * P].rearrange("p (t o) -> p t o", t=T)
        keysT = g_sb[0:RD, 1, T * P:T * P + NE]
        lots = [stage[:, :], res_sb[:, 0, :], res_sb[:, 1, :]]
        N_LOTS = KN + KD // 2

        z_ps = [stack.enter_context(nc.psum_tensor(f"z_ps{i}", [P, HALF], f32)) for i in range(2)]
        t_ps = [stack.enter_context(nc.psum_tensor(f"t_ps{i}", [P, HALF], f32)) for i in range(2)]
        w_ps = [stack.enter_context(nc.psum_tensor(f"w_ps{i}", [P, HALF], f32)) for i in range(4)]

        x_in, c_in, c_in_first, gates_in = sem("x_in"), sem("c_in"), sem("c_in_first"), sem("gates_in")
        wz_in, wt_in = sem("wz_in"), sem("wt_in")
        wp_in, wg_in, keys_in, wq_in, gn_in = sem("wp_in"), sem("wg_in"), sem("keys_in"), sem("wq_in"), sem("gn_in")
        lot_in = sems("lot_in", N_LOTS)
        o_free = sems("o_free", T)
        pool_set, consts, wz_blocks, tanh_done, c_scaled, c_lo_first = (
            sem("pool_set"), sem("consts"), sem("wz_blocks"), sem("tanh_done"), sem("c_scaled"),
            sem("c_lo_first"))
        prep_done, prep_hi, prep_lo = sem("prep_done"), sem("prep_hi"), sem("prep_lo")
        x_var, x_rstd, xt_done, q_done, q_hi_s, q_lo_s = (
            sem("x_var"), sem("x_rstd"), sem("xt_done"), sems("q_done", T), sems("q_hi_s", T), sem("q_lo_s"))
        c_hi_s, c_lo_s = sems("c_hi_s", T), sem("c_lo_s")
        u_done, u_copied = sems("u_done", USES), sems("u_copied", USES)
        g_done, g_copied = sems("g_done", USES), sems("g_copied", USES)
        p_done, p_reduced = sems("p_done", USES), sems("p_reduced", USES)
        u_stats, mean_sum, mean_read = sem("u_stats"), sem("mean_sum"), sem("mean_read")
        va_sum, va_read, y_var, y_rstd = sem("va_sum"), sem("va_read"), sem("y_var"), sem("y_rstd")
        w_var, w_rstd, h_done = sems("w_var", T), sems("w_rstd", T), sems("h_done", 2 * T)
        hT_done, hT_hi_s, hT_lo_s = sems("hT_done", 2 * T), sems("hT_hi_s", 2 * T), sems("hT_lo_s", 2 * T)
        res_done = sem("res_done")
        z_done, max_done, exp_done, zg_done = (
            sems("z_done", T), sems("max_done", T), sems("exp_done", T), sems("zg_done", T))
        zT_done, zT_hi_s, zT_lo_s = sems("zT_done", T), sems("zT_hi_s", T), sems("zT_lo_s", T)
        out_done, out_added = sems("out_done", USES), sems("out_added", USES)
        dve_step = sem("dve_step")

        stack.enter_context(nc.allow_non_contiguous_dma(reason="norm weights and gates: a few hundred bytes"))
        block = stack.enter_context(nc.Block())

        SMALL = ["wz", "keys", "wu", "router", "wg", "wp"]
        A_GROUPS = [("a", n, g) for n in range(KN) for g in range(KD // 4)]
        B_GROUPS = [("b", o, 0) for o in range(KD)]
        LATE_B = USES
        PREP = [(name, 0, 0) for name in SMALL] + A_GROUPS + B_GROUPS
        n_late = len(PREP) - LATE_B
        lot_uses = [("a", n, KD // 4 - 1) for n in range(KN)] + [("b", 2 * o + 1, 0) for o in range(KD // 2)]
        LOT_DONE = [PREP.index(last_use) + 1 for last_use in lot_uses]

        n_first = SMALL.index("wg")
        after_u = [n_first + n for n in (2, 4, 6, 7)]

        def groups_after_u(k):
            return range(n_first if k == 0 else after_u[k - 1], after_u[k])

        def groups_after_pg(k, i):
            n = after_u[-1] + 2 * k + i
            return [n] if n < n_late else []

        assert after_u[-1] + 2 * USES >= n_late
        MEANS_AT = (2, 1)
        assert groups_after_pg(2, 0)[0] % 2 == 1 and groups_after_pg(2, 1)[0] % 2 == 0

        def prep_bank(n):
            return t_ps[n % 2] if n < n_late else w_ps[n - n_late]

        def prep_dest(n):
            kind, i, g = PREP[n]
            ps = prep_bank(n)
            whole = ps[:, 0:half].rearrange("p (t c) -> p t c", t=T)
            if kind == "wp":
                return whole, Wp_hi[:, :, :], Wp_lo[:, :, :]
            if kind == "wg":
                return whole, Wg_hi[:, :, :], Wg_lo[:, :, :]
            if kind == "wu":
                return whole, Wu_hi[:, :, :], Wu_lo[:, :, :]
            if kind == "wz":
                return ps[:, 0:T * P].rearrange("p (t o) -> p t o", t=T), wzT, None
            if kind == "keys":
                return ps[0:RD, 0:NE], keysT, None
            if kind == "router":
                cols = slice(NN, NN + NE)
                return ps[:, :].rearrange("p (k e) -> p k e", k=KD), A_hi[:, :, cols], A_lo[:, :, cols]
            four = ps[:, :].rearrange("p (k n) -> p k n", k=4)
            if kind == "a":
                at = (slice(None), slice(4 * g, 4 * g + 4), slice(i * P, i * P + P))
                return four, A_hi[at], A_lo[at]
            at = (slice(None), slice(0, KN), slice(i * P, i * P + P))
            return four, B_hi[at], B_lo[at]

        @block.sync
        def _(sp):
            sp.dma_start(wz_in_rows, Wz.rearrange("(t p) i -> p t i", p=P)).then_inc(wz_in, 16)
            sp.dma_start(wt_nat, Wt.rearrange("(t p) c -> p t c", p=P)).then_inc(wt_in, 16)
            sp.dma_start(c_sb[:, 0, :], sample(c_v, 0)[:, 0, :]).then_inc(c_in_first, 16)
            sp.dma_start(c_sb[:, 1:T, :], sample(c_v, 0)[:, 1:T, :]).then_inc(c_in, 16)
            sp.dma_start(wg_nat, Wg.rearrange("(t p) c -> p t c", p=P)).then_inc(wg_in, 16)
            sp.dma_start(wp_nat, Wp.rearrange("(t p) c -> p t c", p=P)).then_inc(wp_in, 16)
            sp.dma_start(x_sb[:, :, :], sample(x_v, 0)).then_inc(x_in, 16)

            def load_lot(j):
                place = lots[j % len(lots)]
                if j >= len(lots):
                    sp.wait_ge(prep_done, LOT_DONE[j - len(lots)])
                if j < KN:
                    sp.dma_start(place, a_v[j]).then_inc(lot_in[j], 16)
                else:
                    sp.dma_start(place.rearrange("p (t n) -> p t n", t=2), b_v[j - KN]).then_inc(lot_in[j], 16)

            for j in range(len(lots)):
                load_lot(j)
            sp.dma_start(gates[:, 0:1], g_xattn.partition_broadcast(P)).then_inc(gates_in, 16)
            sp.dma_start(gates[:, 1:2], g_ffn.partition_broadcast(P)).then_inc(gates_in, 16)
            sp.dma_start(gnw[:, :], gn_w.rearrange("(t p) -> p t", p=P)).then_inc(gn_in, 16)
            sp.dma_start(gnb[:, :], gn_b.rearrange("(t p) -> p t", p=P)).then_inc(gn_in, 16)
            for j in range(len(lots), N_LOTS):
                load_lot(j)

            def load(b, n_prev):
                sp.wait_ge(xt_done, n_prev)
                sp.wait_ge(c_lo_s, n_prev)
                sp.dma_start(x_sb[:, :, :], sample(x_v, b)).then_inc(x_in, 16)
                sp.dma_start(c_sb[:, :, :], sample(c_v, b)).then_inc(c_in, 16)

            def store(b, n):
                for t in range(T):
                    sp.wait_ge(out_added[NH * t + NH - 1], n + 1)
                    sp.dma_start(tile_of(o_v, b, t), o_sb[:, t, :]).then_inc(o_free[t], 16)

            load(1, 1)
            with sp.Fori(0, NB - 2) as b:
                load(b + 2, sp.snap(b + 2))
                store(b, b + 1)
            store(NB - 2, NB - 1)
            for k in range(USES):
                t, h = divmod(k, NH)
                cols = slice(h * HALF, (h + 1) * HALF)
                sp.wait_ge(out_added[k], NB + 1)
                sp.dma_start(o_v[NB - 1, t][:, cols], o_sb[:, t, cols]).then_inc(o_free[t], 16)
            for t in range(T):
                sp.wait_ge(o_free[t], 16 * (NB + NH))

        @block.gpsimd
        def _(pool):
            pool.memset(ident[:, :], 0.0).then_inc(pool_set, 1)
            pool.memset(minus_half[:, :], -0.5).then_inc(pool_set, 1)
            pool.wait_ge(pool_set, 2)
            pool.affine_select(out=ident[:, :], in_=ident[:, :], compare_op=ALU.not_equal, fill=1.0,
                               base=0, pattern=[[-1, P]], channel_multiplier=1).then_inc(consts, 1)

            def ctx_low(t, n, prev):
                pool.wait_ge(c_hi_s[t], n)
                if t == 0:
                    pool.wait_ge(p_done[USES - 1], prev)
                return pool.tensor_tensor(c_lo[:, t, :], c_sb[:, t, :], c_hi[:, t, :].bitcast(f32), ALU.subtract)

            def x_root(n):
                pool.wait_ge(x_var, n)
                pool.tensor_tensor(x_rs[:, :], x_ve[:, :], minus_half[:, :], ALU.pow).then_inc(x_rstd, 1)

            def query_low(n):
                for t in range(T):
                    pool.wait_ge(q_hi_s[t], n)
                    last = pool.tensor_tensor(q_lo[:, t, :], ln_sb[:, t, :], q_hi[:, t, :].bitcast(f32),
                                              ALU.subtract)
                last.then_inc(q_lo_s, 1)

            def y_root(n):
                pool.wait_ge(y_var, n)
                pool.tensor_tensor(y_rs[:, :], y_ve[:, :], minus_half[:, :], ALU.pow).then_inc(y_rstd, 1)

            def w_root(t, n):
                pool.wait_ge(w_var[t], n)
                pool.tensor_tensor(w_rs[:, t:t + 1], w_ve[:, t:t + 1], minus_half[:, t:t + 1],
                                   ALU.pow).then_inc(w_rstd[t], 1)

            x_root(1)
            query_low(1)
            pool.wait_ge(x_in, 16)
            for k in range(USES):
                t, h = divmod(k, NH)
                at = (slice(None), t, slice(h * HALF, (h + 1) * HALF))
                pool.wait_ge(c_scaled, k + 1)
                last = pool.tensor_tensor(xt_sb[at], xt_sb[at], x_sb[at], ALU.add)
            last.then_inc(xt_done, 1)
            y_root(1)
            w_root(0, 1)

            def next_attention(n, m):
                ctx_low(0, m, n)
                w_root(1, n)
                ctx_low(1, m, n).then_inc(c_lo_s, 1)
                x_root(m)
                query_low(m)
                y_root(m)
                w_root(0, m)

            with pool.Fori(0, NB - 1) as b:
                next_attention(pool.snap(b + 1), pool.snap(b + 2))
            w_root(1, NB)

        @block.scalar
        def _(act):
            act.dma_start(keys_nat, keys).then_inc(keys_in, 16)
            act.dma_start(wq_nat, Wq).then_inc(wq_in, 16)

            def prep(n):
                src, hi, lo = prep_dest(n)
                act.wait_ge(prep_done, n + 1)
                act.activation(hi, src, ACT.Copy).then_inc(prep_hi, 1)

            def ctx_hi(n, prev):
                if prev is None:
                    act.wait_ge(c_in_first, 16)
                else:
                    act.wait_ge(c_in, act_c_in)
                    act.wait_ge(p_done[USES - 1], prev)
                for t in range(T):
                    if prev is None and t > 0:
                        act.wait_ge(c_in, 16)
                    act.activation(c_hi[:, t, :], c_sb[:, t, :], ACT.Copy).then_inc(c_hi_s[t], 1)

            def query_hi(n):
                for t in range(T):
                    act.wait_ge(q_done[t], n)
                    act.activation(q_hi[:, t, :], ln_sb[:, t, :], ACT.Copy).then_inc(q_hi_s[t], 1)

            def residual(n):
                act.wait_ge(h_done[2 * T - 1], n)
                act.wait_ge(out_added[USES - 1], n)
                for t in range(T):
                    last = act.activation(res_sb[:, t, :], uw_sb[:, t, :], ACT.Identity, bias=shift[:, t:t + 1])
                last.then_inc(res_done, 1)

            def u_copy(k, n):
                t, h = divmod(k, NH)
                act.wait_ge(u_done[k], n)
                act.activation(uw_sb[:, t, h * HALF:(h + 1) * HALF], w_ps[k][:, :], ACT.Copy).then_inc(u_copied[k], 1)

            def g_copy(k, n):
                act.wait_ge(g_done[k], n)
                if k >= 2:
                    act.wait_ge(p_reduced[k - 2], n)
                act.activation(g_sb[:, k % 2, :], w_ps[2 * (k % 2)][:, :], ACT.Copy).then_inc(g_copied[k], 1)

            def hT_high(t, n):
                for g in range(2):
                    k = 2 * t + g
                    act.wait_ge(hT_done[k], n)
                    act.activation(hT_hi[:, t, g * HALF:(g + 1) * HALF], t_ps[g][:, :], ACT.Copy)\
                       .then_inc(hT_hi_s[k], 1)

            def zT_high(t, n):
                act.wait_ge(zT_done[t], n)
                act.activation(zT_hi[:, t, :], t_ps[0][:, :], ACT.Copy).then_inc(zT_hi_s[t], 1)

            def exps(t, n):
                act.wait_ge(max_done[t], n)
                act.activation(ex[:, :], sc[:, :], ACT.Exp, bias=neg_max[:, 0:1]).then_inc(exp_done[t], 1)

            def scale_ctx(k):
                t, h = divmod(k, NH)
                at = (slice(None), t, slice(h * HALF, (h + 1) * HALF))
                if k == 0:
                    act.wait_ge(tanh_done, 1)
                act.activation(xt_sb[at], c_sb[at], ACT.Copy, scale=tg[:, 0:1]).then_inc(c_scaled, 1)

            for n in range(n_first - 1):
                prep(n)
            ctx_hi(1, None)
            prep(n_first - 1)
            for k in range(USES):
                u_copy(k, 1)
                for n in groups_after_u(k):
                    prep(n)
                if k == 1:
                    query_hi(1)
            act.wait_ge(gates_in, 32)
            act.activation(tg[:, :], gates[:, :], ACT.Tanh).then_inc(tanh_done, 1)
            for k in range(USES):
                g_copy(k, 1)
                for i in range(2):
                    for n in groups_after_pg(k, i):
                        prep(n)
                    if k < NH:
                        scale_ctx(2 * k + i)
            for n in range(n_late, len(PREP)):
                prep(n)
            hT_high(0, 1)

            def ffn_and_next(n, m):
                ctx_hi(m, n)
                residual(n)
                hT_high(1, n)
                exps(0, n)
                act.wait_ge(res_done, n)
                for k in range(USES):
                    u_copy(k, m)
                zT_high(0, n)
                query_hi(m)
                exps(1, n)
                for k in range(USES):
                    g_copy(k, m)
                    if k == 2:
                        zT_high(1, n)
                hT_high(0, m)

            with act.Fori(0, NB - 1) as b:
                act_c_in = act.snap(16 * b + 32)
                ffn_and_next(act.snap(b + 1), act.snap(b + 2))
            hT_high(1, NB)
            residual(NB)
            exps(0, NB)
            zT_high(0, NB)
            exps(1, NB)
            zT_high(1, NB)

        @block.vector
        def _(dve):
            steps = [0]

            def step(instruction):
                instruction.then_inc(dve_step, 1)
                steps[0] += 1

            def settle():
                dve.wait_ge(dve_step, steps[0])

            def fresh_steps():
                settle()
                dve.sem_clear(dve_step)
                steps[0] = 0

            def prep(n):
                src, hi, lo = prep_dest(n)
                dve.wait_ge(prep_hi, n + 1)
                if lo is None:
                    dve.engine_nop().then_inc(prep_lo, 1)
                    return
                last = dve.tensor_tensor(lo, src, hi.bitcast(f32), ALU.subtract)
                if n < n_late:
                    last.then_inc(prep_lo, 1)
                else:
                    last.then_inc(out_added[n - n_late], 1)

            def x_stats(n, n_dma):
                dve.wait_ge(x_in, n_dma)
                for t in range(T):
                    for h in range(NH):
                        step(dve.bn_stats(x_st[:, t, 6 * h:6 * h + 6], x_sb[:, t, h * HALF:(h + 1) * HALF]))
                settle()
                for t in range(T):
                    step(dve.bn_aggr(x_mv[:, t, :], x_st[:, t, :]))
                settle()
                dve.tensor_scalar(x_ve[:, :], x_mv[:, :, 1], EPS, None, ALU.add).then_inc(x_var, 1)

            def x_plus_ctx(n, n_dma):
                dve.wait_ge(c_in, n_dma)
                for t in range(T):
                    last = dve.scalar_tensor_tensor(xt_sb[:, t, :], c_sb[:, t, :], tg[:, 0:1], x_sb[:, t, :],
                                                    ALU.mult, ALU.add)
                last.then_inc(xt_done, 1)

            def query(n, prev):
                dve.wait_ge(x_rstd, n)
                if prev is not None:
                    dve.wait_ge(hT_done[2 * T - 1], prev)
                for t in range(T):
                    dve.tensor_scalar(ln_sb[:, t, :], x_sb[:, t, :], x_mv[:, t, 0:1], x_rs[:, t:t + 1],
                                      ALU.subtract, ALU.mult).then_inc(q_done[t], 1)

            def gate(t, n, banks=z_ps):
                dve.wait_ge(z_done[t], n)
                step(dve.tensor_copy(sc[:, :], banks[1][:, ZH - NE:ZH]))
                settle()
                step(dve.max(top_a[:, :], sc[:, :]))
                settle()
                dve.tensor_scalar(neg_max[:, :], top_a[:, 0:1], -1.0, None, ALU.mult).then_inc(max_done[t], 1)
                step(dve.match_replace(sc1[:, :], top_a[:, :], sc[:, :], TAKEN))
                settle()
                step(dve.max(top_b[:, :], sc1[:, :]))
                settle()
                step(dve.match_replace(sc2[:, :], top_b[:, :], sc1[:, :], TAKEN))
                settle()
                dve.wait_ge(exp_done[t], n)
                step(dve.scalar_tensor_tensor(eg[:, :], sc2[:, :], TAKEN, ex[:, :], ALU.is_equal, ALU.mult,
                                              accum_out=g_sum[:, :]))
                settle()
                step(dve.reciprocal(g_rec[:, :], g_sum[:, :]))
                settle()
                for i, (e, k) in enumerate(((0, E0), (E0, E1))):
                    last = dve.scalar_tensor_tensor(
                        zg_sb[:, t, e * RANK:(e + k) * RANK].rearrange("p (e r) -> p e r", r=RANK),
                        banks[i][:, 0:k * RANK].rearrange("p (e r) -> p e r", r=RANK), g_rec[:, :],
                        eg[:, e:e + k].unsqueeze(2).to_broadcast([P, k, RANK]), ALU.mult, ALU.mult)
                last.then_inc(zg_done[t], 1)

            def hT_low_part(t, g, n):
                k = 2 * t + g
                at = (slice(None), t, slice(g * HALF, (g + 1) * HALF))
                dve.wait_ge(hT_hi_s[k], n)
                dve.tensor_tensor(hT_lo[at], t_ps[g][:, :], hT_hi[at].bitcast(f32), ALU.subtract)\
                   .then_inc(hT_lo_s[k], 1)

            def hT_low(t, n):
                for g in range(2):
                    hT_low_part(t, g, n)

            def zT_low(t, n):
                dve.wait_ge(zT_hi_s[t], n)
                dve.tensor_tensor(zT_lo[:, t, :], t_ps[0][:, :], zT_hi[:, t, :].bitcast(f32), ALU.subtract)\
                   .then_inc(zT_lo_s[t], 1)

            def u_statistics(n, halfway=lambda: None):
                for k in range(USES):
                    if k == NH:
                        halfway()
                    t, h = divmod(k, NH)
                    dve.wait_ge(u_copied[k], n)
                    step(dve.bn_stats(u_st[:, t, 6 * h:6 * h + 6], uw_sb[:, t, h * HALF:(h + 1) * HALF]))
                settle()
                for t in range(T):
                    last = dve.bn_aggr(u_mv[:, t, :], u_st[:, t, :])
                last.then_inc(u_stats, 1)

            def group_deviation(n):
                dve.wait_ge(mean_sum, n)
                dve.tensor_copy(g_mean[:, :], t_ps[1][:, 0:T]).then_inc(mean_read, 1)
                dve.wait_ge(mean_read, n)
                step(dve.tensor_tensor(u_dev[:, :], u_mv[:, :, 0], g_mean[:, :], ALU.subtract))
                settle()
                step(dve.tensor_tensor(a2[:, :], u_dev[:, :], u_dev[:, :], ALU.mult))
                settle()
                step(dve.tensor_tensor(att_var[:, T:2 * T], a2[:, :], u_mv[:, :, 1], ALU.add))

            def reduce_pg(k, n):
                t, h = divmod(k, NH)
                into = att_half[:, t:t + 1] if h == 0 else att_var[:, t:t + 1]
                dve.wait_ge(g_copied[k], n)
                if h > 0:
                    dve.wait_ge(p_reduced[k - 1], n)
                dve.wait_ge(p_done[k], n)
                dve.tensor_tensor_reduce(out=g_sb[:, k % 2, :], in0=w_ps[2 * (k % 2) + 1][:, :],
                                         in1=g_sb[:, k % 2, :], scale=1.0,
                                         scalar=0.0 if h == 0 else att_half[:, t:t + 1],
                                         op0=ALU.mult, op1=ALU.add, accum_out=into).then_inc(p_reduced[k], 1)

            def slopes(n):
                dve.wait_ge(va_sum, n)
                dve.tensor_copy(va[:, :], t_ps[1][:, 0:2 * T]).then_inc(va_read, 1)
                dve.wait_ge(va_read, n)
                step(dve.scalar_tensor_tensor(a2[:, :], va[:, 0:T], float(GROUP * GROUP), va[:, 0:T],
                                              ALU.mult, ALU.mult))
                step(dve.scalar_tensor_tensor(att[:, :], va[:, 0:T], float(GROUP), gnw_t[:, :],
                                              ALU.mult, ALU.mult))
                settle()
                for t in range(T):
                    last = dve.tensor_scalar(y_ve[:, t:t + 1], a2[:, t:t + 1], va[:, T + t:T + t + 1], EPS,
                                             ALU.mult, ALU.add)
                last.then_inc(y_var, 1)
                dve.wait_ge(y_rstd, n)
                step(dve.tensor_tensor(slope[:, :], att[:, :], y_rs[:, :], ALU.mult))
                settle()

            def w_tile(t, meanwhile=None):
                step(dve.scalar_tensor_tensor(uw_sb[:, t, :], uw_sb[:, t, :], slope[:, t:t + 1], xt_sb[:, t, :],
                                              ALU.mult, ALU.add))
                settle()
                for h in range(NH):
                    if meanwhile:
                        meanwhile(h)
                    step(dve.bn_stats(w_st[:, t, 6 * h:6 * h + 6], uw_sb[:, t, h * HALF:(h + 1) * HALF]))
                settle()
                step(dve.bn_aggr(w_mv[:, t, :], w_st[:, t, :]))
                settle()
                dve.tensor_scalar(w_ve[:, t:t + 1], w_mv[:, t, 1:2], EPS, None, ALU.add).then_inc(w_var[t], 1)

            def shifts():
                step(dve.tensor_tensor(shift[:, :], g_mean[:, :], slope[:, :], ALU.mult))
                settle()
                step(dve.tensor_tensor(shift[:, :], gnb_t[:, :], shift[:, :], ALU.subtract))

            def h_tile(t, n):
                dve.wait_ge(w_rstd[t], n)
                dve.wait_ge(q_lo_s, n)
                for h in range(NH):
                    cols = slice(h * HALF, (h + 1) * HALF)
                    dve.tensor_scalar(ln_sb[:, t, cols], uw_sb[:, t, cols], w_mv[:, t, 0:1], w_rs[:, t:t + 1],
                                      ALU.subtract, ALU.mult).then_inc(h_done[NH * t + h], 1)

            def finish_attention(n, add=lambda k: None):
                slopes(n)
                w_tile(0)
                shifts()
                add(0)
                h_tile(0, n)
                add(1)
                w_tile(1, lambda g: hT_low_part(0, g, n))
                add(2)
                h_tile(1, n)
                add(3)

            def add_out(k, n, n_dma):
                t, h = divmod(k, NH)
                cols = slice(h * HALF, (h + 1) * HALF)
                if h == 0:
                    dve.wait_ge(o_free[t], n_dma)
                if k == 0:
                    dve.wait_ge(res_done, n)
                dve.wait_ge(out_done[k], n)
                dve.scalar_tensor_tensor(o_sb[:, t, cols], w_ps[k][:, :], tg2[:, 0:1], res_sb[:, t, cols],
                                         ALU.mult, ALU.add).then_inc(out_added[k], 1)

            step(dve.memset(wz_nat, 0.0))
            step(dve.memset(group_mean[:, :], 0.0))
            settle()
            for g in range(GPT):
                rows = slice(g * GROUP, g * GROUP + GROUP)
                dve.memset(group_mean[rows, rows], 1.0 / GROUP).then_inc(consts, 1)
            dve.wait_ge(wz_in, 16)
            for g in range(GPT):
                rows = slice(g * GROUP, g * GROUP + GROUP)
                last = dve.tensor_copy(wz_nat[rows, :, rows], wz_in_rows[rows, :, :])
            last.then_inc(wz_blocks, 1)
            for n in range(n_first - 1):
                prep(n)
            for t in range(T):
                dve.wait_ge(c_hi_s[t], 1)
                dve.tensor_tensor(c_lo[:, t, :], c_sb[:, t, :], c_hi[:, t, :].bitcast(f32), ALU.subtract)\
                   .then_inc(c_lo_first if t == 0 else c_lo_s, 1)
            prep(n_first - 1)
            x_stats(1, 16)
            for k in range(USES):
                for n in groups_after_u(k):
                    prep(n)
                if k == 0:
                    query(1, None)
            for n in groups_after_pg(0, 0):
                prep(n)

            def second_group():
                for n in groups_after_pg(0, 1):
                    prep(n)

            u_statistics(1, second_group)
            dve.wait_ge(gn_in, 32)
            dve.wait_ge(tanh_done, 1)
            step(dve.tensor_scalar(gnw_t[:, :], gnw[:, :], tg[:, 0:1], None, ALU.mult))
            step(dve.tensor_scalar(gnb_t[:, :], gnb[:, :], tg[:, 0:1], None, ALU.mult))
            step(dve.tensor_scalar(tg2[:, :], tg[:, 1:2], FFN_SCALE, None, ALU.mult))
            for k in range(USES):
                if k > 0:
                    for n in groups_after_pg(k, 0):
                        prep(n)
                reduce_pg(k, 1)
                if k == MEANS_AT[0]:
                    group_deviation(1)
                if k > 0:
                    for n in groups_after_pg(k, 1):
                        prep(n)
            dve.wait_ge(xt_done, 1)

            def late_groups(k):
                for n in {2: range(n_late, len(PREP) - 1), 3: [len(PREP) - 1]}.get(k, []):
                    prep(n)

            finish_attention(1, late_groups)
            fresh_steps()

            def ffn_and_next(n, m, n_dma, m_dma):
                x_stats(m, m_dma)
                hT_low(1, n)
                gate(0, n)
                query(m, n)
                x_plus_ctx(m, m_dma)
                u_statistics(m)
                zT_low(0, n)
                gate(1, n)
                group_deviation(m)
                for k in range(USES):
                    reduce_pg(k, m)
                    if k == 1:
                        zT_low(1, n)
                finish_attention(m, lambda k: add_out(k, n, n_dma))
                fresh_steps()

            with dve.Fori(0, NB - 1) as b:
                ffn_and_next(dve.snap(b + 1), dve.snap(b + 2), dve.snap(16 * b + 16), dve.snap(16 * b + 32))
            hT_low(1, NB)
            gate(0, NB)
            zT_low(0, NB)
            gate(1, NB, w_ps[NH:USES])
            for k in range(USES):
                add_out(k, NB, 16 * NB)
                if k == 0:
                    zT_low(1, NB)

        @block.tensor
        def _(pe):
            def prep(n):
                kind, i, g = PREP[n]
                ps = prep_bank(n)
                if n >= n_late:
                    k = n - n_late
                    pe.wait_ge(g_copied[USES - 2 + k // 2] if k % 2 == 0 else p_reduced[USES - 2 + k // 2], 1)
                elif n >= 2:
                    pe.wait_ge(prep_lo, n - 1)
                if kind in ("wp", "wg"):
                    nat, arrived = (wp_nat, wp_in) if kind == "wp" else (wg_nat, wg_in)
                    pe.wait_ge(arrived, 16)
                    for o in range(T):
                        for c in range(T):
                            last = pe.transpose(ps[:, c * C + o * P:c * C + o * P + P],
                                                nat[:, o, c * P:c * P + P], ident[:, :])
                elif kind == "wz":
                    pe.wait_ge(wz_blocks, 1)
                    for o in range(T):
                        last = pe.transpose(ps[:, o * P:o * P + P], wz_nat[:, o, :], ident[:, :])
                elif kind == "wu":
                    pe.wait_ge(wt_in, 16)
                    pe.wait_ge(prep_hi, SMALL.index("wz") + 1)
                    for o in range(T):
                        for c in range(T):
                            last = pe.matmul(ps[:, c * C + o * P:c * C + o * P + P],
                                             wt_nat[:, o, c * P:c * P + P], wzT[:, o, :], start=True, stop=True)
                elif kind == "keys":
                    pe.wait_ge(keys_in, 16)
                    last = pe.transpose(ps[0:RD, 0:NE], keys_nat, ident[0:NE, 0:NE])
                elif kind == "router":
                    pe.wait_ge(wq_in, 16)
                    pe.wait_ge(prep_hi, SMALL.index("keys") + 1)
                    for k in range(KD):
                        last = pe.matmul(ps[:, k * NE:k * NE + NE], wq_nat[:, k * P:k * P + P], keysT,
                                         start=True, stop=True)
                elif kind == "a":
                    pe.wait_ge(lot_in[i], 16)
                    for k in range(4):
                        d = (4 * g + k) * P
                        last = pe.transpose(ps[:, k * P:k * P + P], lots[i % len(lots)][:, d:d + P], ident[:, :])
                else:
                    j = KN + i // 2
                    pe.wait_ge(lot_in[j], 16)
                    for k in range(KN):
                        at = (i % 2) * NN + k * P
                        last = pe.transpose(ps[:, k * P:k * P + P], lots[j % len(lots)][:, at:at + P], ident[:, :])
                last.then_inc(prep_done, 1)

            def product(ps, w_hi, w_lo, v_hi, v_lo, k, ins, second_tile=None):
                t, h = divmod(k, NH)
                rows, cols = slice(t * P, t * P + P), slice(h * HALF, (h + 1) * HALF)
                passes = [(w, v, c) for c in range(T) for w, v in ((w_hi, v_hi), (w_hi, v_lo), (w_lo, v_hi))]
                for i, (w, v, c) in enumerate(passes):
                    if second_tile and i == len(passes) // T:
                        second_tile()
                    last = pe.matmul(ps, w[:, c, rows], v[:, c, cols], start=(i == 0), stop=(i == len(passes) - 1))
                last.then_inc(ins, 1)

            def u_product_first(between):
                pe.wait_ge(c_lo_first, 1)
                for k in range(USES):
                    product(w_ps[k][:, :], Wu_hi, Wu_lo, c_hi, c_lo, k, u_done[k],
                            (lambda: pe.wait_ge(c_lo_s, 1)) if k == 0 else None)
                    between(k)

            def pg_products(n, between):
                for k in range(USES):
                    first = 2 * (k % 2)
                    pe.wait_ge(u_copied[first] if k < 2 else g_copied[k - 2], n)
                    product(w_ps[first][:, :], Wg_hi, Wg_lo, c_hi, c_lo, k, g_done[k])
                    between(k, 0)
                    if k == 0:
                        pe.wait_ge(q_lo_s, n)
                    pe.wait_ge(u_copied[first + 1] if k < 2 else p_reduced[k - 2], n)
                    product(w_ps[first + 1][:, :], Wp_hi, Wp_lo, q_hi, q_lo, k, p_done[k])
                    between(k, 1)

            def group_means(n):
                pe.wait_ge(u_stats, n)
                pe.matmul(t_ps[1][:, 0:T], group_mean[:, :], u_mv[:, :, 0], start=True, stop=True)\
                  .then_inc(mean_sum, 1)

            def group_att_var(n):
                pe.wait_ge(mean_read, n)
                pe.wait_ge(p_reduced[USES - 1], n)
                pe.matmul(t_ps[1][:, 0:2 * T], group_mean[:, :], att_var[:, :], start=True, stop=True)\
                  .then_inc(va_sum, 1)

            def hT(t, n):
                for g in range(2):
                    pe.wait_ge(h_done[2 * t + g], n)
                    for k in range(4):
                        d = (4 * g + k) * P
                        last = pe.transpose(t_ps[g][:, k * P:k * P + P], ln_sb[:, t, d:d + P], ident[:, :])
                    last.then_inc(hT_done[2 * t + g], 1)
                    if g == 0:
                        pe.wait_ge(va_read if t == 0 else hT_lo_s[1], n)

            def z_product(t, n, middle=None, banks=z_ps):
                for k in range(KD):
                    if k % 4 == 0:
                        pe.wait_ge(hT_lo_s[2 * t + k // 4], n)
                    row = slice(k * P, k * P + P)
                    for h, w in ((hT_hi, A_hi), (hT_hi, A_lo), (hT_lo, A_hi)):
                        for i in range(2):
                            last = pe.matmul(banks[i][:, 0:ZH], h[:, t, row], w[:, k, i * ZH:(i + 1) * ZH],
                                             start=(k == 0 and h is hT_hi and w is A_hi),
                                             stop=(k == KD - 1 and h is hT_lo))
                    if k == 3 and middle:
                        middle()
                last.then_inc(z_done[t], 1)

            def zT(t, n):
                pe.wait_ge(zg_done[t], n)
                for k in range(KN):
                    last = pe.transpose(t_ps[0][:, k * P:k * P + P], zg_sb[:, t, k * P:k * P + P], ident[:, :])
                last.then_inc(zT_done[t], 1)

            def out_product(k, n, middle=None):
                t, h = divmod(k, NH)
                cols = slice(h * HALF, (h + 1) * HALF)
                pe.wait_ge(zT_lo_s[t], n)
                for j in range(KN):
                    row = slice(j * P, j * P + P)
                    for z, w in ((zT_hi, B_hi), (zT_hi, B_lo), (zT_lo, B_hi)):
                        last = pe.matmul(w_ps[k][:, :], z[:, t, row], w[:, j, cols],
                                         start=(j == 0 and z is zT_hi and w is B_hi),
                                         stop=(j == KN - 1 and z is zT_lo))
                    if j == KN // 2 - 1 and middle:
                        middle()
                last.then_inc(out_done[k], 1)

            for t in range(T):
                pe.sem_inc(o_free[t], 16)
            pe.wait_ge(consts, 1 + GPT)
            for n in range(n_first):
                prep(n)

            def prep_after_u(k):
                for n in groups_after_u(k):
                    prep(n)

            u_product_first(prep_after_u)

            def prep_after_pg(k, i):
                if (k, i) == MEANS_AT:
                    pe.wait_ge(prep_lo, groups_after_pg(2, 0)[-1] + 1)
                    group_means(1)
                if (k, i) == (3, 0):
                    pe.wait_ge(mean_read, 1)
                for n in groups_after_pg(k, i):
                    prep(n)

            pg_products(1, prep_after_pg)
            pe.wait_ge(prep_lo, n_late)
            group_att_var(1)
            for n in range(n_late, len(PREP)):
                prep(n)
            hT(0, 1)

            def ffn_and_next(n, m):
                def second_tile():
                    pe.wait_ge(hT_lo_s[0], n)
                    hT(1, n)

                z_product(0, n, second_tile)
                u_product_next(n, m)
                pe.wait_ge(hT_lo_s[2], n)
                zT(0, n)
                pe.wait_ge(zg_done[0], n)
                z_product(1, n)
                pe.wait_ge(hT_lo_s[3], n)
                group_means(m)

                def between(k, i):
                    if (k, i) == (2, 0):
                        pe.wait_ge(zT_lo_s[0], n)
                        zT(1, n)

                pg_products(m, between)
                pe.wait_ge(g_copied[2], m)
                out_product(0, n, lambda: group_att_var(m))
                pe.wait_ge(p_reduced[2], m)
                out_product(1, n)
                pe.wait_ge(g_copied[3], m)
                out_product(2, n)
                pe.wait_ge(zT_lo_s[1], n)
                hT(0, m)
                pe.wait_ge(p_reduced[3], m)
                out_product(3, n)

            def u_product_next(n, m):
                pe.wait_ge(c_lo_s, m)
                for k in range(USES):
                    pe.wait_ge(out_added[k], n)
                    product(w_ps[k][:, :], Wu_hi, Wu_lo, c_hi, c_lo, k, u_done[k])

            with pe.Fori(0, NB - 1) as b:
                ffn_and_next(pe.snap(b + 1), pe.snap(b + 2))

            def last_second_tile():
                pe.wait_ge(hT_lo_s[0], NB)
                hT(1, NB)

            z_product(0, NB, last_second_tile)
            for k in range(NH, USES):
                pe.wait_ge(out_added[k], NB)

            def first_gated():
                pe.wait_ge(hT_lo_s[2], NB)
                zT(0, NB)

            z_product(1, NB, first_gated, banks=w_ps[NH:USES])
            for k in range(NH):
                pe.wait_ge(out_added[k], NB)
                out_product(k, NB, (lambda: zT(1, NB)) if k == 1 else None)
            for k in range(NH, USES):
                out_product(k, NB)


INPUTS = ["x", "ctx_4096", "g_xattn", "g_ffn", "L0_xattn_Wt", "L0_xattn_Wp", "L0_xattn_Wg", "L0_xattn_Wz",
          "L0_xattn_gn_w", "L0_xattn_gn_b", "L0_ffn_A_w", "L0_ffn_B_w", "L0_ffn_Wq_w", "L0_ffn_keys"]


def kernel(**inputs):
    import numpy as np
    import concourse.bacc as bacc
    from concourse.bass_utils import run_bass_kernel_spmd

    nc = bacc.Bacc("TRN2", target_bir_lowering=False, num_devices=1)
    arrays, views = {}, []
    for name in INPUTS:
        a = np.ascontiguousarray(inputs[name])
        arrays[f"in_{name}"] = a
        views.append(nc.dram_tensor(f"in_{name}", a.shape, mybir.dt.from_np(a.dtype), kind="ExternalInput").ap())
    shape = inputs["x"].shape
    out = nc.dram_tensor("out_block", shape, mybir.dt.float32, kind="ExternalOutput").ap()
    flamingo_block(nc, *views, out)
    result = run_bass_kernel_spmd(nc, [arrays], core_ids=[0])
    return result.results[0]["out_block"]
```
